# Optimizing a Trainium2 kernel written in Bass

```python
import numpy as np
import jax
import jax.numpy as jnp

def _softmax(x, axis=-1):
    return jax.nn.softmax(x, axis=axis)

def _gelu(x):
    return jax.nn.gelu(x, approximate=True)

def _silu(x):
    return jax.nn.silu(x)

def _sigmoid(x):
    return jax.nn.sigmoid(x)

def _layernorm(x, axis=-1, eps=1e-05):
    m = jnp.mean(x, axis=axis, keepdims=True)
    v = jnp.var(x, axis=axis, keepdims=True)
    return (x - m) / jnp.sqrt(v + eps)

def _scatter_add(tgt, idx, src, axis=0):
    return tgt.at[idx].add(src)

def _segment_sum(src, seg, n):
    return jax.ops.segment_sum(src, seg, n)
kernel_name = 'mk_pixart_resid_d1_seqx_r4_c5c29e'

def setup_inputs(seed: int=0):
    np.random.seed(seed)
    _w = jnp.asarray

    def _rec_inputs():
        import jax
        import jax.numpy as jnp
        _rk = jax.random.key(seed)
        x = -0.0002928 + 1 * jax.random.normal(jax.random.fold_in(_rk, 1), (8, 256, 512), jnp.float32)
        _lenS = 256 - jax.random.randint(jax.random.fold_in(_rk, 7), (8,), 0, max(1, 256 // 4) + 1, jnp.int32)
        _lenS2 = 256 - jax.random.randint(jax.random.fold_in(_rk, 8), (8,), 0, max(1, 256 // 4) + 1, jnp.int32)
        _ctx_2048P = jax.random.normal(jax.random.fold_in(_rk, 11), (8, 16, 512), jnp.float32)
        _ctx_2048c = jax.random.dirichlet(jax.random.fold_in(_rk, 511), 0.3 * jnp.ones((16,), jnp.float32), (8, 256))
        _ctx_2048t = jnp.einsum('bsk,bkd->bsd', _ctx_2048c, _ctx_2048P)
        _ctx_2048t = _ctx_2048t * jax.lax.rsqrt(jnp.mean(jnp.square(_ctx_2048t)) + 1e-12) * 0.953939
        ctx_2048 = -1.39393e-06 + 0.999914 * (_ctx_2048t + 0.3 * jax.random.normal(jax.random.fold_in(_rk, 611), (8, 256, 512), jnp.float32))
        itok_B_779_1933 = jax.random.randint(jax.random.fold_in(_rk, 12), (8,), 779, 1934, jnp.int32)
        return (x, ctx_2048, itok_B_779_1933)
    x, ctx_2048, itok_B_779_1933 = _rec_inputs()

    def _L0_xcond_setup():
        import jax, jax.numpy as jnp
        import numpy as np
        NUM_HEADS = 8
        HEAD_DIM = 64
        AVG_K_LENGTH = 20
        SCALE = 1.0 / (HEAD_DIM ** 0.5 * float(np.log(AVG_K_LENGTH)))
        key = jax.random.key(seed)
        k1, k2, k3, k4 = jax.random.split(key, 4)
        B, HD, LQ, LK = (4, NUM_HEADS * HEAD_DIM, 512, 512)
        q = jax.random.normal(k1, (B, HD, LQ), dtype=jnp.float32)
        k = jax.random.normal(k2, (B, HD, LK), dtype=jnp.float32)
        v = jax.random.normal(k3, (B, HD, LK), dtype=jnp.float32)
        k_length = jax.random.randint(k4, (B,), 128, LK + 1, dtype=jnp.int32)
        return {'q': q, 'k': k, 'v': v, 'k_length': k_length}
    _L0_xcond_all = _L0_xcond_setup()
    _L0_xcond_in = {k: v for k, v in _L0_xcond_all.items() if k in ()}
    del _L0_xcond_all

    def _L0_ffn_setup():
        import jax, jax.numpy as jnp
        import numpy as np
        from jax import lax
        DIM = 512
        E = 8
        K = 2
        RANK = 32
        CAP_FACTOR = 1.25

        def gelu(x):
            return jax.nn.gelu(x, approximate=False)

        def _moe_forward(x, gate_w, w1, b1, w2, b2, wd, wu, sw1, sb1, sw2, sb2, swd, swu):
            B, S, D = x.shape
            T = B * S
            cap = max(1, int(T * CAP_FACTOR / E))
            xt = x.reshape(T, D)
            logits = xt @ gate_w
            probs_full = jax.nn.softmax(logits, axis=-1)
            top_p, top_i = lax.top_k(probs_full, K)
            out = jnp.zeros_like(xt)
            for k in range(K):
                e = top_i[:, k]
                w = top_p[:, k]
                onehot = jax.nn.one_hot(e, E, dtype=jnp.int32)
                pos_all = jnp.cumsum(onehot, axis=0) - 1
                pos = jnp.take_along_axis(pos_all, e[:, None], axis=1)[:, 0]
                keep = pos < cap
                pos_c = jnp.where(keep, pos, cap)
                buf = jnp.zeros((E, cap, D), x.dtype).at[e, pos_c].set(xt * keep[:, None].astype(x.dtype), mode='drop')
                h = gelu(jnp.einsum('ecd,edf->ecf', buf, w1) + b1[:, None, :])
                y = jnp.einsum('ecf,efd->ecd', h, w2) + b2[:, None, :]
                a = jnp.einsum('ecr,erd->ecd', gelu(jnp.einsum('ecd,edr->ecr', buf, wd)), wu)
                y = y + a
                tok = y[e, jnp.minimum(pos_c, cap - 1)]
                out = out + tok * keep[:, None].astype(x.dtype) * w[:, None]
            sh = gelu(xt @ sw1 + sb1) @ sw2 + sb2
            sh = sh + gelu(xt @ swd) @ swu
            out = out + 0.2 * sh
            return out.reshape(B, S, D)
        key = jax.random.key(seed)
        ks = jax.random.split(key, 16)
        s = 0.02
        d, h = (DIM, 4 * DIM)
        inp = {'x': jax.random.normal(ks[0], (4, 512, d), dtype=jnp.float32), 'gate_w': jax.random.normal(ks[1], (d, E), dtype=jnp.float32) * s, 'w1': jax.random.normal(ks[2], (E, d, h), dtype=jnp.float32) * s, 'b1': jnp.zeros((E, h), dtype=jnp.float32), 'w2': jax.random.normal(ks[3], (E, h, d), dtype=jnp.float32) * s, 'b2': jnp.zeros((E, d), dtype=jnp.float32), 'wd': jax.random.normal(ks[4], (E, d, RANK), dtype=jnp.float32) * s, 'wu': jax.random.normal(ks[5], (E, RANK, d), dtype=jnp.float32) * s, 'sw1': jax.random.normal(ks[6], (d, h), dtype=jnp.float32) * s, 'sb1': jnp.zeros((h,), dtype=jnp.float32), 'sw2': jax.random.normal(ks[7], (h, d), dtype=jnp.float32) * s, 'sb2': jnp.zeros((d,), dtype=jnp.float32), 'swd': jax.random.normal(ks[8], (d, RANK), dtype=jnp.float32) * s, 'swu': jax.random.normal(ks[9], (RANK, d), dtype=jnp.float32) * s}
        return inp
    _L0_ffn_all = _L0_ffn_setup()
    _L0_ffn_in = {k: v for k, v in _L0_ffn_all.items() if k in ('gate_w', 'w1', 'b1', 'w2', 'b2', 'wd', 'wu', 'sw1', 'sb1', 'sw2', 'sb2', 'swd', 'swu')}
    del _L0_ffn_all
    return {'x': x, 'ctx_2048': ctx_2048, 'itok_B_779_1933': itok_B_779_1933, 'L0_ffn_gate_w': _L0_ffn_in['gate_w'], 'L0_ffn_w1': _L0_ffn_in['w1'], 'L0_ffn_b1': _L0_ffn_in['b1'], 'L0_ffn_w2': _L0_ffn_in['w2'], 'L0_ffn_b2': _L0_ffn_in['b2'], 'L0_ffn_wd': _L0_ffn_in['wd'], 'L0_ffn_wu': _L0_ffn_in['wu'], 'L0_ffn_sw1': _L0_ffn_in['sw1'], 'L0_ffn_sb1': _L0_ffn_in['sb1'], 'L0_ffn_sw2': _L0_ffn_in['sw2'], 'L0_ffn_sb2': _L0_ffn_in['sb2'], 'L0_ffn_swd': _L0_ffn_in['swd'], 'L0_ffn_swu': _L0_ffn_in['swu']}

def reference(x, ctx_2048, itok_B_779_1933, L0_ffn_gate_w, L0_ffn_w1, L0_ffn_b1, L0_ffn_w2, L0_ffn_b2, L0_ffn_wd, L0_ffn_wu, L0_ffn_sw1, L0_ffn_sb1, L0_ffn_sw2, L0_ffn_sb2, L0_ffn_swd, L0_ffn_swu):
    import jax
    import jax.numpy as jnp

    def _L0_xcond_ref(q, k, v, k_length):
        import jax, jax.numpy as jnp
        import numpy as np
        NUM_HEADS = 8
        HEAD_DIM = 64
        AVG_K_LENGTH = 20
        SCALE = 1.0 / (HEAD_DIM ** 0.5 * float(np.log(AVG_K_LENGTH)))
        b, hd, lq = q.shape
        lk = k.shape[-1]
        d = hd // NUM_HEADS
        qh = q.reshape(b, NUM_HEADS, d, lq)
        kh = k.reshape(b, NUM_HEADS, d, lk)
        vh = v.reshape(b, NUM_HEADS, d, lk)
        s = SCALE * jnp.log(k_length.astype(jnp.float32))[:, None, None, None]
        attn = jnp.einsum('bhdq,bhdk->bhqk', qh, kh)
        attn = jax.nn.softmax(s * attn, axis=-1)
        out = jnp.einsum('bhqk,bhdk->bhdq', attn, vh)
        return out.reshape(b, hd, lq)

    def _L0_ffn_ref(x, gate_w, w1, b1, w2, b2, wd, wu, sw1, sb1, sw2, sb2, swd, swu):
        import jax, jax.numpy as jnp
        import numpy as np
        from jax import lax
        DIM = 512
        E = 8
        K = 2
        RANK = 32
        CAP_FACTOR = 1.25

        def gelu(x):
            return jax.nn.gelu(x, approximate=False)

        def _moe_forward(x, gate_w, w1, b1, w2, b2, wd, wu, sw1, sb1, sw2, sb2, swd, swu):
            B, S, D = x.shape
            T = B * S
            cap = max(1, int(T * CAP_FACTOR / E))
            xt = x.reshape(T, D)
            logits = xt @ gate_w
            probs_full = jax.nn.softmax(logits, axis=-1)
            top_p, top_i = lax.top_k(probs_full, K)
            out = jnp.zeros_like(xt)
            for k in range(K):
                e = top_i[:, k]
                w = top_p[:, k]
                onehot = jax.nn.one_hot(e, E, dtype=jnp.int32)
                pos_all = jnp.cumsum(onehot, axis=0) - 1
                pos = jnp.take_along_axis(pos_all, e[:, None], axis=1)[:, 0]
                keep = pos < cap
                pos_c = jnp.where(keep, pos, cap)
                buf = jnp.zeros((E, cap, D), x.dtype).at[e, pos_c].set(xt * keep[:, None].astype(x.dtype), mode='drop')
                h = gelu(jnp.einsum('ecd,edf->ecf', buf, w1) + b1[:, None, :])
                y = jnp.einsum('ecf,efd->ecd', h, w2) + b2[:, None, :]
                a = jnp.einsum('ecr,erd->ecd', gelu(jnp.einsum('ecd,edr->ecr', buf, wd)), wu)
                y = y + a
                tok = y[e, jnp.minimum(pos_c, cap - 1)]
                out = out + tok * keep[:, None].astype(x.dtype) * w[:, None]
            sh = gelu(xt @ sw1 + sb1) @ sw2 + sb2
            sh = sh + gelu(xt @ swd) @ swu
            out = out + 0.2 * sh
            return out.reshape(B, S, D)
        return _moe_forward(x, gate_w, w1, b1, w2, b2, wd, wu, sw1, sb1, sw2, sb2, swd, swu)
    x = x + _L0_xcond_ref(_layernorm(x, axis=-1), ctx_2048, ctx_2048, itok_B_779_1933)
    x = x + _L0_ffn_ref(_layernorm(x, axis=-1), L0_ffn_gate_w, L0_ffn_w1, L0_ffn_b1, L0_ffn_w2, L0_ffn_b2, L0_ffn_wd, L0_ffn_wu, L0_ffn_sw1, L0_ffn_sb1, L0_ffn_sw2, L0_ffn_sb2, L0_ffn_swd, L0_ffn_swu)
    return x

_drawn_inputs = setup_inputs


def setup_inputs(seed=0):
    import zlib

    import numpy as np

    out = dict(_drawn_inputs(seed))
    spreads = {'L0_ffn_b1': (0.0, 0.734),
     'L0_ffn_b2': (0.0, 0.387),
     'L0_ffn_sb1': (0.0, 0.8),
     'L0_ffn_sb2': (0.0, 0.545)}
    factors = {'L0_ffn_wd': 8.0, 'L0_ffn_wu': 8.0, 'L0_ffn_swd': 8.0, 'L0_ffn_swu': 8.0}
    for name, (base, spread) in spreads.items():
        noise = np.random.default_rng([zlib.crc32(name.encode()), seed]).standard_normal(out[name].shape)
        drawn = base * np.exp(spread * noise) if base else spread * noise
        out[name] = jnp.asarray(drawn.astype(out[name].dtype))
    for name, factor in factors.items():
        out[name] = (out[name] * factor).astype(out[name].dtype)
    return out
```

```python
from contextlib import ExitStack

import concourse.bass as bass
from concourse import mybir

import numpy as np

F32 = mybir.dt.float32
BF16 = mybir.dt.bfloat16
I32 = mybir.dt.int32
ALU = mybir.AluOpType
ACT = mybir.ActivationFunctionType
X_AXIS = mybir.AxisListType.X

P = 128
B, C, L = 8, 256, 512
T, D = B * C, L
HEADS, HD = 8, 32
GROUPS = T // P
GH = P // HD
QT = L // P
SCALE = 1.0 / (64 ** 0.5 * float(np.log(20)))
EPS = 1e-5
E, TOPK, RANK = 8, 2, 32
F = 4 * D
CAP = int(T * 1.25 / E)
SLOTS = TOPK * CAP
CH = SLOTS // P
KB, FB = D // P, F // P
PASS = 256
GPP = PASS // P
DROPPED = 1 << 14
WIDE = RANK * 3


class Signal:

    def __init__(self, sem, step):
        self.sem, self.step, self.value = sem, step, 0

    def now(self):
        return self, self.value


class Queue:

    def __init__(self):
        self.items, self.passed = [], {}

    def wait(self, *marks):
        for signal, value in marks:
            if self.passed.get(signal, 0) < value:
                self.passed[signal] = value
                self.items.append((None, signal.sem, value, None))

    def do(self, instruction, *args, done=None, **kwargs):
        self.items.append((instruction, args, kwargs, done))
        if done is not None:
            done.value += done.step
            return done.now()

    def issue(self, engine):
        for instruction, a, b, done in self.items:
            if instruction is None:
                engine.wait_ge(a, b)
            else:
                issued = instruction(*a, **b)
                if done is not None:
                    issued.then_inc(done.sem, done.step)


def build(nc, x, ctx_in, itok, gate_w, w1, b1, w2, b2, wd, wu, sw1, sb1, sw2, sb2, swd, swu, out):
    stack = ExitStack()
    with stack:
        def sb(name, shape, dt):
            return stack.enter_context(nc.sbuf_tensor(name, shape, dt))

        def signal(name, step=1):
            return Signal(stack.enter_context(nc.semaphore(name)), step)

        def dma_signal(name):
            return signal(name, 16)

        pe, act, dve, pool, sp = Queue(), Queue(), Queue(), Queue(), Queue()
        mm, tr = nc.tensor.matmul, nc.tensor.transpose
        dv, ac, gp = nc.vector, nc.scalar, nc.gpsimd

        x_rows = x.rearrange("b c l -> (b c) l")
        ctx_rows = ctx_in.rearrange("b c l -> (b c) l")
        xn_rows = nc.dram_tensor("normed_rows", [T + P, 2 * D], BF16, kind="Internal").ap()
        table = nc.dram_tensor("slot_table", [E * SLOTS, 2], I32, kind="Internal").ap()

        w1h, w1l = sb("w1h", [P, KB, F], BF16), sb("w1l", [P, KB, F], BF16)
        w2h, w2l = sb("w2h", [P, FB, D], BF16), sb("w2l", [P, FB, D], BF16)
        wdf = sb("wdf", [P, KB, RANK], F32)
        wdh, wdl = sb("wdh", [P, KB, WIDE], BF16), sb("wdl", [P, KB, WIDE], BF16)
        wuf, wus = sb("wuf", [WIDE, D], F32), sb("wus", [P, D], BF16)
        hidden = sb("hidden", [P, 2 * FB * SLOTS], BF16)
        hh, hl = (hidden[:, k * FB * SLOTS:(k + 1) * FB * SLOTS].rearrange("p (f n) -> p f n", n=SLOTS) for k in range(2))
        hf = [sb(f"hf{i}", [P, SLOTS], F32) for i in range(2)]
        low = [sb(f"low{i}", [P, SLOTS], BF16) for i in range(2)]
        lowf = sb("lowf", [WIDE, SLOTS], F32)
        yout = [sb(f"yout{i}", [P, D], F32) for i in range(3)]
        ident = sb("ident", [P, P], F32)
        identb = sb("identb", [P, P], BF16)
        before = sb("before", [P, P], BF16)
        ones = sb("ones", [P, P], BF16)
        half = sb("half", [P, 1], F32)
        b1rows, b1cols = sb("b1rows", [P, P], F32), sb("b1cols", [P, E * FB], F32)
        sb1rows, sb1cols = sb("sb1rows", [FB, P], F32), sb("sb1cols", [P, FB], F32)
        b2f = sb("b2f", [E + 1, D], F32)
        b2parts = sb("b2parts", [E + 1, 3, D], BF16)
        gate = sb("gate", [P, KB, E], F32)
        logits = sb("logits", [P, GROUPS, E], F32)
        slots = sb("slots", [P, E, CH, 2], I32)

        base = nc.sbuf_base
        offset = [base + (-base) % 64]
        region_start = offset[0]
        limit = nc.sbuf_usable_end

        def at(name, shape, dt, size):
            n = size
            for s in shape[1:]:
                n *= s
            t = nc.alloc_sbuf_tensor_at(name, shape, dt, offset=offset[0])
            offset[0] += n + (-n) % 64
            if offset[0] > limit:
                raise ValueError(f"{name} ends at {offset[0]}, {limit} is the limit")
            return t

        xth = [at(f"xth{i}", [P, KB, PASS], BF16, 2) for i in range(2)]
        xtl = [at(f"xtl{i}", [P, KB, PASS], BF16, 2) for i in range(2)]
        NX, NS = 4, 4
        xin = [at(f"xin{i}", [P, L], F32, 4) for i in range(NX)]
        cin = [at(f"cin{i}", [P, L], F32, 4) for i in range(2)]
        xn = at("xn", [P, L], F32, 4)
        routing_start = offset[0]
        QS = [at(f"QS{i}", [P, GH, L], BF16, 2) for i in range(NS)]
        KS = [at(f"KS{i}", [P, GH, L], BF16, 2) for i in range(NS)]
        VT = [at(f"VT{i}", [P, 2, QT, P], BF16, 2) for i in range(2)]
        prob = [at(f"prob{i}", [P, L], F32, 4) for i in range(3)]
        shh, shl = (hidden[:, k * FB * PASS:(k + 1) * FB * PASS].rearrange("p (f n) -> p f n", n=PASS) for k in range(2))
        NPH = 8
        spare = hidden[:, 2 * FB * PASS:2 * FB * PASS + 2 * NPH * L].rearrange("p (n l) -> p n l", l=L)
        ph = [spare[:, i, :] for i in range(NPH)]
        pl = [spare[:, NPH + i, :] for i in range(NPH)]
        split = [hidden[:, 2 * FB * PASS + (2 * NPH + 4 * i) * L:][:, 0:4 * L].rearrange("p (n l) -> p n l", l=L) for i in range(2)]
        rowmax = [at(f"rowmax{i}", [P, GH * QT], F32, 4) for i in range(2)]
        MS = at("MS", [P, GH * QT, HD], BF16, 2)
        rden = at("rden", [P, L], F32, 4)
        x2s = [at(f"x2_{i}", [P, L], F32, 4) for i in range(2)]
        x2r = [at(f"x2r{i}", [P, 2, L], BF16, 2) for i in range(2)]
        x2t = at("x2t", [P, KB, P], F32, 4)
        stat = at("stat", [P, 2, 6], F32, 4)
        mv = at("mv", [P, 2, 4], F32, 4)
        scale_i = at("scale_i", [P, B], I32, 4)
        scale_f = at("scale_f", [P, B], F32, 4)
        scales = at("scales", [P, B], F32, 4)

        offset[0] = region_start
        NST = 3
        stage = [at(f"stage{i}", [P, 2048], F32, 4) for i in range(NST)]
        xg = at("xg", [P, CH, 2 * D], BF16, 2)
        eth = [at(f"eth{i}", [P, KB, SLOTS], BF16, 2) for i in range(2)]
        etl = [at(f"etl{i}", [P, KB, SLOTS], BF16, 2) for i in range(2)]
        PB = stack.enter_context(nc.psum_tensor("banks", [P, 8, 512], F32))

        def bank(i):
            return PB[:, i, :]

        s_const = signal("s_const")
        s_pool = signal("s_pool")
        s_dve = signal("s_dve")
        s_act = signal("s_act")
        s_small = dma_signal("s_small")

        def fill(view, value):
            pool.do(gp.memset, view, value, done=s_pool)
            pool.wait(s_pool.now())

        small = []
        small.append(sp.do(nc.sync.dma_start, scale_i[:, :], itok.rearrange("(a b) -> a b", a=1).partition_broadcast(P).rearrange("p a b -> p (a b)"), done=s_small))
        small.append(sp.do(nc.sync.dma_start, gate[:, :, :], gate_w.rearrange("(k p) e -> p k e", p=P), done=s_small))
        small.append(sp.do(nc.sync.dma_start, b1rows[:, :], b1.rearrange("e (c p) -> (e c) p", p=P), done=s_small))
        small.append(sp.do(nc.sync.dma_start, sb1rows[:, :], sb1.rearrange("(c p) -> c p", p=P), done=s_small))
        small.append(sp.do(nc.sync.dma_start, b2f[0:E, :], b2, done=s_small))
        small.append(sp.do(nc.sync.dma_start, b2f[E:E + 1, :], sb2.rearrange("(a d) -> a d", a=1), done=s_small))
        loaded_small = small[-1]

        fill(ident[:, :], 0.0)
        pool.do(gp.affine_select, out=ident[:, :], in_=ident[:, :], compare_op=ALU.not_equal, fill=1.0,
                base=0, pattern=[[-1, P]], channel_multiplier=1, done=s_pool)
        pool.wait(s_pool.now())
        pool.do(gp.tensor_copy, identb[:, :], ident[:, :], done=s_const)
        fill(before[:, :], 0.0)
        pool.do(gp.affine_select, out=before[:, :], in_=before[:, :], compare_op=ALU.is_ge, fill=1.0,
                base=0, pattern=[[-1, P]], channel_multiplier=1, done=s_const)
        pool.wait(s_const.now())
        fill(ones[:, :], 1.0)
        fill(half[:, :], -0.5)
        fill(MS[:, :, :], 0.0)
        fill(wus[96:P, :], 0.0)
        for i in range(2):
            fill(low[i][96:P, :], 1.0)
        for i in range(NS):
            fill(KS[i][96:P, :, :], 1.0)
        constants = s_pool.now()
        for queue in (dve, pe, act):
            queue.wait(s_const.now(), constants)

        s_scale = signal("s_scale")
        dve.wait(loaded_small)
        m = dve.do(dv.tensor_copy, scale_f[:, :], scale_i[:, :], done=s_dve)
        act.wait(m)
        m = act.do(ac.activation, scales[:, :], scale_f[:, :], ACT.Ln, done=s_act)
        dve.wait(m)
        m_scale = dve.do(dv.tensor_scalar, scales[:, :], scales[:, :], SCALE, None, ALU.mult, done=s_scale)
        act.wait(m_scale)
        def step(*args, **kwargs):
            mark = dve.do(*args, done=s_dve, **kwargs)
            dve.wait(mark)
            return mark

        step(dv.tensor_copy, b2parts[:, 0, :], b2f[:, :])
        step(dv.tensor_tensor, b2f[:, :], b2f[:, :], b2parts[:, 0, :], ALU.subtract)
        step(dv.tensor_copy, b2parts[:, 1, :], b2f[:, :])
        m_b2 = step(dv.tensor_tensor, b2parts[:, 2, :], b2f[:, :], b2parts[:, 1, :], ALU.subtract)
        s_bias = signal("s_bias")
        s_biasc = signal("s_biasc")
        pe.wait(loaded_small)
        pe.do(tr, bank(3)[:, 0:P], b1rows[:, :], ident[:, :])
        m = pe.do(tr, bank(3)[:, P:P + FB], sb1rows[:, :], ident[0:FB, 0:FB], done=s_bias)
        dve.wait(m)
        dve.do(dv.tensor_copy, b1cols[:, :], bank(3)[:, 0:P], done=s_biasc)
        m_biascols = dve.do(dv.tensor_copy, sb1cols[:, :], bank(3)[:, P:P + FB], done=s_biasc)
        act.wait(m_biascols)

        s_x = [dma_signal(f"s_x{i}") for i in range(NX)]
        s_c = [dma_signal(f"s_c{i}") for i in range(2)]
        s_rstd = signal("s_rstd")
        s_split = signal("s_split")
        s_khi = signal("s_khi")
        s_stack = [dma_signal(f"s_stack{i}") for i in range(NS)]
        s_vt, s_vtc = signal("s_vt"), signal("s_vtc")
        s_S, s_max = signal("s_S"), signal("s_max")
        s_ms, s_mrow, s_mrowc = signal("s_ms"), signal("s_mrow"), signal("s_mrowc")
        s_ST, s_exp, s_ph, s_pl, s_pv = (signal(n) for n in ("s_ST", "s_exp", "s_ph", "s_pl", "s_pv"))
        s_out = signal("s_out")
        s_x1st = [dma_signal(f"s_x1st{i}") for i in range(2)]
        s_x2, s_x2r = signal("s_x2hi"), signal("s_x2lo")
        s_x2st = [dma_signal(f"s_x2st{i}") for i in range(2)]
        s_x2t, s_x2tc = signal("s_x2t"), signal("s_x2tc")
        s_gate, s_logit, s_xt = signal("s_gate"), signal("s_logit"), signal("s_xt")

        x_loaded, c_loaded, split_done, khi_done, stacked, vt_done = {}, {}, {}, {}, {}, {}
        s_released, st_done, mrow_done, out_done, x1_stored, x2_stored = {}, {}, {}, {}, {}, {}
        xt_ready = {}
        bank_free = {i: m_biascols for i in range(8)}

        def layer_norm(src, dst, k, src_marks):
            dve.wait(*src_marks)
            step(dv.bn_stats, stat[:, k, :], src)
            step(dv.bn_aggr, mv[:, k, 0:2], stat[:, k, :])
            m = step(dv.tensor_scalar, mv[:, k, 2:3], mv[:, k, 1:2], EPS, None, ALU.add)
            pool.wait(m)
            m = pool.do(gp.tensor_tensor, mv[:, k, 3:4], mv[:, k, 2:3], half[:, :], ALU.pow, done=s_rstd)
            dve.wait(m)
            return step(dv.tensor_scalar, dst, src, mv[:, k, 0:1], mv[:, k, 3:4], ALU.subtract, ALU.mult)

        def load_group(g):
            rows = slice(P * g, P * g + P)
            if g >= NX:
                sp.wait(x2_done[g - NX], x1_stored[g - NX])
            x_loaded[g] = sp.do(nc.sync.dma_start, xin[g % NX][:, :], x_rows[rows, :], done=s_x[g % NX])
            if g >= 2:
                sp.wait(split_done[g - 2], khi_done[g - 2])
            c_loaded[g] = sp.do(nc.sync.dma_start, cin[g % 2][:, :], ctx_rows[rows, :], done=s_c[g % 2])

        def prepare(g):
            s, part = g % NS, split[g % 2]
            if g >= 2:
                dve.wait(stacked[g - 2])
                act.wait(stacked[g - 2])
                act.wait(vt_done[g - 2])
                dve.wait(vt_done[g - 2])
            layer_norm(xin[g % NX][:, :], xn[:, :], 0, [x_loaded[g]])
            step(dv.tensor_copy, part[:, 0, :], xn[:, :])
            dve.do(dv.tensor_tensor, part[:, 1, :], xn[:, :], part[:, 0, :], ALU.subtract, done=s_split)
            act.wait(c_loaded[g])
            khi_done[g] = act.do(ac.activation, part[:, 2, :], cin[g % 2][:, :], ACT.Copy, done=s_khi)
            dve.wait(khi_done[g], c_loaded[g])
            split_done[g] = dve.do(dv.tensor_tensor, part[:, 3, :], cin[g % 2][:, :], part[:, 2, :],
                                   ALU.subtract, done=s_split)
            if g >= NS:
                sp.wait(st_done[g - NS])
            sp.wait(split_done[g], khi_done[g])
            for h in range(GH):
                rows = slice(HD * h, HD * h + HD)
                for dst, parts in ((QS[s], (0, 1, 0)), (KS[s], (2, 2, 3))):
                    for k, which in enumerate(parts):
                        sp.do(nc.sync.dma_start, dst[HD * k:HD * k + HD, h, :], part[rows, which, :], done=s_stack[s])
            stacked[g] = s_stack[s].now()

        def transpose_values(g, b):
            pe.wait(split_done[g], khi_done[g], bank_free[b])
            view = bank(b).bitcast(BF16)
            for k in range(2):
                for t in range(QT):
                    at_ = (k * QT + t) * P
                    pe.do(tr, view[:, at_:at_ + P], split[g % 2][:, 2 + k, t * P:t * P + P], identb[:, :],
                          done=s_vt if (k, t) == (1, QT - 1) else None)
            vt_done[g] = s_vt.now()
            act.wait(vt_done[g])
            if g >= 2:
                act.wait(pv_done[g - 2])
            bank_free[b] = act.do(ac.activation, VT[g % 2][:, :, :, :].rearrange("p a t c -> p (a t c)"), view[:, :],
                                  ACT.Copy, done=s_vtc)
            vtc_done[g] = bank_free[b]

        pv_done, vtc_done = {}, {}

        def score_max(g, i, b):
            h, t = divmod(i, QT)
            s = g % NS
            pe.wait(stacked[g], bank_free[b])
            m = pe.do(mm, bank(b), QS[s][0:96, h, t * P:t * P + P], KS[s][0:96, h, :], start=True, stop=True, done=s_S)
            dve.wait(m)
            bank_free[b] = dve.do(dv.reduce_max, rowmax[g % 2][:, i:i + 1], bank(b), X_AXIS, done=s_max)

        def max_rows(g, b):
            s = g % NS
            dve.wait(s_max.now())
            if g:
                dve.wait(mrow_done[g - 1])
            mx = rowmax[g % 2][:, :]
            step(dv.tensor_scalar, MS[:, :, 0], mx, -1.0, None, ALU.mult)
            m = dve.do(dv.scalar_tensor_tensor, MS[:, :, 1], mx, -1.0, MS[:, :, 0], ALU.mult, ALU.subtract, done=s_ms)
            pe.wait(m, bank_free[b])
            for t in range(QT):
                for h in range(GH):
                    last = (t, h) == (QT - 1, GH - 1)
                    pe.do(mm, bank(b)[HD * h:HD * h + HD, t * P:t * P + P], MS[:, h * QT + t, :], identb[:, :],
                          start=True, stop=True, done=s_mrow if last else None)
            mrow_done[g] = s_mrow.now()
            act.wait(mrow_done[g])
            for h in range(GH):
                act.do(ac.activation, QS[s][96:P, h, :], bank(b)[HD * h:HD * h + HD, :], ACT.Copy, done=s_mrowc)
            bank_free[b] = s_mrowc.now()
            mrowc_done[g] = bank_free[b]

        mrowc_done = {}
        tick = {"st": 0}
        ph_mark, pl_mark, ph_read = {}, {}, {}

        def exponentials(g, i, b):
            t, h = divmod(i, GH)
            s, n = g % NS, tick["st"]
            tick["st"] += 1
            pe.wait(stacked[g], mrowc_done[g], bank_free[b])
            m = pe.do(mm, bank(b), KS[s][:, h, t * P:t * P + P], QS[s][:, h, :], start=True, stop=True, done=s_ST)
            act.wait(m)
            if n >= 3:
                act.wait(ph_mark[n - 3], pl_mark[n - 3])
            m = act.do(ac.activation, prob[n % 3][:, :], bank(b), ACT.Exp, scale=scales[:, g // 2:g // 2 + 1], done=s_exp)
            bank_free[b] = m
            if n >= NPH:
                act.wait(ph_read[n - NPH])
                pool.wait(ph_read[n - NPH])
            act.wait(m)
            ph_mark[n] = act.do(ac.activation, ph[n % NPH], prob[n % 3][:, :], ACT.Copy, done=s_ph)
            pool.wait(ph_mark[n], m)
            pl_mark[n] = pool.do(gp.tensor_tensor, pl[n % NPH], prob[n % 3][:, :], ph[n % NPH],
                                 ALU.subtract, done=s_pl)
            if i == GH * QT - 1:
                st_done[g] = s_ST.now()

        def weighted_values(g, t, b_out, b_sum):
            n0 = g * GH * QT + t * GH
            v = VT[g % 2]
            pe.wait(vtc_done[g], ph_mark[n0 + GH - 1], pl_mark[n0 + GH - 1])
            if t == 0:
                pe.wait(bank_free[b_out], bank_free[b_sum])
            work = [(b_sum, None, ph), (b_out, 0, ph), (b_out, 1, ph), (b_sum, None, pl), (b_out, 0, pl)]
            opened = set()
            for k, (b, part, src) in enumerate(work):
                for h in range(GH):
                    cols = slice(HD * h, HD * h + HD)
                    lhsT = ones[:, 0:HD] if part is None else v[:, part, t, cols]
                    last = (k, h) == (len(work) - 1, GH - 1)
                    pe.do(mm, bank(b)[cols, :], lhsT, src[(n0 + h) % NPH],
                          start=t == 0 and b not in opened, stop=t == QT - 1 and k >= 3, done=s_pv if last else None)
                opened.add(b)
            for h in range(GH):
                ph_read[n0 + h] = s_pv.now()
            if t == QT - 1:
                pv_done[g] = s_pv.now()

        def finish_attention(g, b_out, b_sum):
            rows = slice(P * g, P * g + P)
            dve.wait(pv_done[g])
            step(dv.reciprocal, rden[:, :], bank(b_sum))
            bank_free[b_sum] = s_dve.now()
            o = xin[g % NX]
            step(dv.tensor_tensor, rden[:, :], bank(b_out), rden[:, :], ALU.mult)
            bank_free[b_out] = s_dve.now()
            out_done[g] = dve.do(dv.tensor_tensor, o[:, :], o[:, :], rden[:, :], ALU.add, done=s_out)
            sp.wait(out_done[g])
            x1_stored[g] = sp.do(nc.sync.dma_start, out[rows, :], o[:, :], done=s_x1st[g % 2])
            x2 = x2s[g % 2]
            if g >= 2:
                dve.wait(x2t_done[g - 2])
            m = layer_norm(o[:, :], x2[:, :], 1, [out_done[g]])
            x2_done[g] = m
            if g >= 2:
                act.wait(x2_stored[g - 2])
                dve.wait(x2_stored[g - 2])
            r = x2r[g % 2]
            act.wait(m)
            m = act.do(ac.activation, r[:, 0, :], x2[:, :], ACT.Copy, done=s_x2)
            dve.wait(m)
            m = dve.do(dv.tensor_tensor, r[:, 1, :], x2[:, :], r[:, 0, :], ALU.subtract, done=s_x2r)
            sp.wait(m)
            x2_stored[g] = sp.do(nc.sync.dma_start, xn_rows[rows, :], r[:, :, :].rearrange("p a d -> p (a d)"), done=s_x2st[g % 2])

        x2t_done, x2_done = {}, {}

        def transpose_tokens(g, b):
            p, col = g // GPP, (g % GPP) * P
            x2 = x2s[g % 2]
            pe.wait(x2_done[g], bank_free[b])
            for k in range(KB):
                pe.do(tr, bank(b)[:, k * P:k * P + P], x2[:, k * P:k * P + P], ident[:, :], done=s_x2t if k == KB - 1 else None)
            x2t_done[g] = s_x2t.now()
            act.wait(x2t_done[g])
            if g:
                act.wait(xt_ready[g - 1], gate_done[g - 1])
            m = act.do(ac.activation, x2t[:, :, :].rearrange("p k t -> p (k t)"), bank(b), ACT.Copy, done=s_x2tc)
            pe.wait(m)
            for k in range(KB):
                pe.do(mm, bank(b)[:, 0:E], x2t[:, k, :], gate[:, k, :], start=k == 0, stop=k == KB - 1,
                      done=s_gate if k == KB - 1 else None)
            gate_done[g] = s_gate.now()
            hi, lo = xth[p % 2][:, :, col:col + P], xtl[p % 2][:, :, col:col + P]
            dve.wait(m)
            if p >= 2:
                dve.wait(pass_up_done[p - 2])
            step(dv.tensor_copy, hi, x2t[:, :, :])
            xt_ready[g] = dve.do(dv.tensor_tensor, lo, x2t[:, :, :], hi, ALU.subtract, done=s_xt)
            dve.wait(gate_done[g])
            bank_free[b] = dve.do(dv.tensor_copy, logits[:, g, :], bank(b)[:, 0:E], done=s_logit)

        gate_done, pass_up_done = {}, {}

        s_up, s_gelu, s_hh, s_hl = signal("s_up"), signal("s_gelu"), signal("s_hh"), signal("s_hl")
        s_down, s_y = signal("s_down"), signal("s_y")
        s_yst = [dma_signal(f"s_yst{i}") for i in range(3)]
        count = {"up": 0, "down": 0, "rank": 0}
        gelu_mark, h_split, low_done, y_stored = {}, {}, {}, {}
        low_read = {}
        last_down = [constants]
        w1_ready, w2_ready, wd_ready, wu_ready = {}, {}, {}, {}

        def rank_features(x_hi, x_lo, halves, units):
            n = count["rank"]
            count["rank"] += 1
            b0 = units[count["up"] % len(units)]
            count["up"] += 1
            pe.wait(wd_ready["now"], *[bank_free[b0 + j] for j in range(len(halves))])
            for j, (c0, w) in enumerate(halves):
                k = 0
                for weights, data in ((wdh, x_hi), (wdh, x_lo), (wdl, x_hi)):
                    for kb in range(KB):
                        k += 1
                        pe.do(mm, bank(b0 + j)[0:WIDE, 0:w], weights[:, kb, :], data[:, kb, c0:c0 + w],
                              start=k == 1, stop=k == 3 * KB, done=s_up if (j, k) == (len(halves) - 1, 3 * KB) else None)
            act.wait(s_up.now())
            w, total = halves[0][1], sum(w for _, w in halves)
            if n:
                act.wait(low_done[n - 1])
            m = act.do(ac.activation, lowf[:, 0:total].rearrange("p (j w) -> p j w", w=w), PB[0:WIDE, b0:b0 + len(halves), 0:w],
                       ACT.Gelu, done=s_gelu)
            for j in range(len(halves)):
                bank_free[b0 + j] = m
            o = low[n % 2]
            dve.wait(m)
            if n >= 2:
                dve.wait(low_read[n - 2])
            step(dv.tensor_copy, o[0:WIDE, 0:total], lowf[:, 0:total])
            low_done[n] = step(dv.tensor_tensor, o[HD:2 * HD, 0:total], lowf[HD:2 * HD, 0:total], o[HD:2 * HD, 0:total], ALU.subtract)
            return n

        def up_block(x_hi, x_lo, halves, fb, units, bias, hh, hl):
            n = count["up"]
            count["up"] += 1
            b0 = units[n % len(units)]
            pe.wait(w1_ready["now"][fb // 4], *[bank_free[b0 + j] for j in range(len(halves))])
            f0 = fb * P
            k = 0
            for weights, data in ((w1h, x_hi), (w1h, x_lo), (w1l, x_hi)):
                for kb in range(KB):
                    k += 1
                    for j, (c0, w) in enumerate(halves):
                        pe.do(mm, bank(b0 + j)[:, 0:w], weights[:, kb, f0:f0 + P], data[:, kb, c0:c0 + w],
                              start=k == 1, stop=k == 3 * KB, done=s_up if (j, k) == (len(halves) - 1, 3 * KB) else None)
            act.wait(s_up.now())
            w, total = halves[0][1], sum(w for _, w in halves)
            if n - 2 in h_split:
                act.wait(h_split[n - 2])
            m = act.do(ac.activation, hf[n % 2][:, 0:total].rearrange("p (j w) -> p j w", w=w),
                       PB[:, b0:b0 + len(halves), 0:w], ACT.Gelu, bias=bias, done=s_gelu)
            for j in range(len(halves)):
                bank_free[b0 + j] = m
            dve.wait(m, last_down[0])
            dve.wait(dve.do(dv.tensor_copy, hh[:, fb, 0:total], hf[n % 2][:, 0:total], done=s_hh))
            h_split[n] = dve.do(dv.tensor_tensor, hl[:, fb, 0:total], hf[n % 2][:, 0:total], hh[:, fb, 0:total],
                                ALU.subtract, done=s_hl)
            return n

        def down_chunk(c, first_up, rank_n, ybanks, store, hh, hl):
            n = count["down"]
            count["down"] += 1
            b = ybanks[n % len(ybanks)]
            cols = slice(c * P, c * P + P)
            pe.wait(bank_free[b], low_done[rank_n], wu_ready["now"])
            pe.do(mm, bank(b), low[rank_n % 2][:, cols], wus[:, :], start=True, stop=False)
            for fb in range(FB):
                pe.wait(h_split[first_up + fb], w2_ready["now"][fb // 4])
                for k, (a, w) in enumerate(((hh, w2h), (hh, w2l), (hl, w2h))):
                    last = (fb, k) == (FB - 1, 2)
                    pe.do(mm, bank(b), a[:, fb, cols], w[:, fb, :], start=False, stop=last, done=s_down if last else None)
                yield
            last_down[0] = s_down.now()
            act.wait(last_down[0])
            if n >= 3:
                act.wait(y_stored[n - 3])
            bank_free[b], y_stored[n] = store(n, b)

        s_stage = [dma_signal(f"s_stage{i}") for i in range(NST)]
        s_wd, s_wu = dma_signal("s_wd"), dma_signal("s_wu")
        s_rankb = dma_signal("s_rankb")
        s_whi, s_wlo = signal("s_whi"), signal("s_wlo")
        count["stage"] = 0
        stage_free = {}

        def split_weights(stages, src, dst_hi, dst_lo, written_over):
            n = count["stage"]
            count["stage"] += 1
            i = n % len(stages)
            sp.wait(*stage_free.get(i, []))
            a, w = src.shape[1], src.shape[2]
            buf = stages[i].rearrange("p (a w) -> p a w", w=w)
            m = sp.do(nc.sync.dma_start, buf, src, done=s_stage[i])
            act.wait(m, written_over)
            hi = act.do(ac.activation, dst_hi, buf, ACT.Copy, done=s_whi)
            dve.wait(m, hi, written_over)
            lo = dve.do(dv.tensor_tensor, dst_lo, buf, dst_hi, ALU.subtract, done=s_wlo)
            stage_free[i] = [hi, lo]
            return lo

        def w1_quarter(stages, w, q, written_over):
            cols = slice(q * 512, q * 512 + 512)
            return split_weights(stages, w.rearrange("(k p) f -> p k f", p=P)[:, :, cols], w1h[:, :, cols], w1l[:, :, cols], written_over)

        def w2_quarter(stages, w, q, written_over):
            rows = slice(q * 4, q * 4 + 4)
            return split_weights(stages, w.rearrange("(k p) d -> p k d", p=P)[:, rows, :], w2h[:, rows, :], w2l[:, rows, :], written_over)

        def rank_down_weights(w, written_over):
            sp.wait(written_over, *stage_free.get("wd", []))
            m = sp.do(nc.sync.dma_start, wdf[:, :, :], w.rearrange("(k p) r -> p k r", p=P), done=s_wd)
            dve.wait(m, written_over)
            for j in range(3):
                step(dv.tensor_copy, wdh[:, :, j * RANK:(j + 1) * RANK], wdf[:, :, :])
            for j in range(3):
                step(dv.tensor_tensor, wdl[:, :, j * RANK:(j + 1) * RANK], wdf[:, :, :], wdh[:, :, j * RANK:(j + 1) * RANK], ALU.subtract)
            stage_free["wd"] = [s_dve.now()]
            wd_ready["now"] = s_dve.now()

        def rank_up_weights(w, bias_row, written_over):
            sp.wait(written_over, m_b2, *stage_free.get("wu", []))
            for j in range(3):
                sp.do(nc.sync.dma_start, wuf[j * RANK:(j + 1) * RANK, :], w, done=s_wu)
            wu_loaded = s_wu.now()
            for j in range(3):
                sp.do(nc.sync.dma_start, wus[96 + j:97 + j, :], b2parts[bias_row:bias_row + 1, j, :], done=s_rankb)
            dve.wait(wu_loaded, written_over)
            step(dv.tensor_copy, wus[0:WIDE, :], wuf[:, :])
            m = step(dv.tensor_tensor, wus[64:96, :], wuf[64:96, :], wus[64:96, :], ALU.subtract)
            stage_free["wu"] = [m]
            dve.wait(s_rankb.now())
            wu_ready["now"] = m
            pe.wait(s_rankb.now())

        hstage = [hidden[:, k * FB * PASS:(k + 1) * FB * PASS].bitcast(F32) for k in range(2)]

        def shared_weights():
            w1_ready["now"], w2_ready["now"] = [], []
            for q in range(4):
                w1_ready["now"].append(w1_quarter(hstage, sw1, q, constants))
                yield
            for q in range(4):
                w2_ready["now"].append(w2_quarter(hstage, sw2, q, constants))
                yield
            rank_down_weights(swd, constants)
            rank_up_weights(swu, E, constants)
            yield

        added = {}

        def store_shared(p, c):
            def store(n, b):
                y = yout[n % 3]
                m = act.do(ac.activation, y[:, :], bank(b), ACT.Copy, scale=0.2, done=s_y)
                rows = slice((p * GPP + c) * P, (p * GPP + c) * P + P)
                pool.wait(m, x1_stored[p * GPP + c])
                return m, pool.do(gp.dma_start, out[rows, :], y[:, :], accum_op=ALU.add, done=s_yst[n % 3])
            return store

        FFN_BANKS = [6, 7]
        pass_state = {}

        def shared_up(p):
            hi, lo = xth[p % 2], xtl[p % 2]
            pe.wait(*[xt_ready[p * GPP + i] for i in range(GPP)])
            halves = [(0, PASS)]
            r = rank_features(hi, lo, halves, FFN_BANKS)
            pass_state[p] = (count["up"], r)
            yield
            for fb in range(FB):
                up_block(hi, lo, halves, fb, FFN_BANKS, sb1cols[:, fb:fb + 1], shh, shl)
                yield
            pass_up_done[p] = s_up.now()

        def shared_down(p):
            first, r = pass_state[p]
            for c in range(GPP):
                yield from down_chunk(c, first, r, FFN_BANKS, store_shared(p, c), shh, shl)
            low_read[r] = last_down[0]

        def without_exponentials(w):
            if w >= 1:
                finish_attention(2 * w - 1, *PV_BANKS[1])
            for g in (2 * w + 2, 2 * w + 3):
                if g < GROUPS:
                    load_group(g)
            for k, g in enumerate((2 * w, 2 * w + 1)):
                if g < GROUPS:
                    transpose_values(g, 3)
                for i in range(GH * QT):
                    if g < GROUPS:
                        score_max(g, i, i % 2)
                    if i == 4 and w >= 1:
                        transpose_tokens(g - 2, 2)
                    if i % 2:
                        yield
                if g < GROUPS:
                    max_rows(g, 3)

        def with_exponentials(w):
            for k, g in enumerate((2 * w, 2 * w + 1)):
                for i in range(GH * QT):
                    exponentials(g, i, i % 2)
                    if i % GH == GH - 1 and i >= 2 * GH - 1:
                        weighted_values(g, i // GH - 1, *PV_BANKS[k])
                    if i == 2 and k == 1:
                        finish_attention(g - 1, *PV_BANKS[0])
                    if i == 8 and g + 2 < GROUPS:
                        prepare(g + 2)
                    if i == 12:
                        next(weights, None)
                    yield
                weighted_values(g, QT - 1, *PV_BANKS[k])

        def together(main, other, ratio):
            owed = 0.0
            for _ in main:
                owed += ratio
                while owed >= 1:
                    owed -= 1
                    next(other, None)
            for _ in other:
                pass

        PV_BANKS = [(4, 5), (2, 3)]
        weights = shared_weights()
        load_group(0)
        load_group(1)
        prepare(0)
        prepare(1)
        LAST = GROUPS // 2
        for w in range(LAST + 2):
            p = w - 2
            up = shared_up(p) if p >= 0 else iter(())
            down = shared_down(p) if p >= 0 else iter(())
            if p == 0:
                for _ in weights:
                    pass
            together(without_exponentials(w) if w <= LAST else iter(()), up, 17 / 16)
            together(with_exponentials(w) if w < LAST else iter(()), down, 1)

        offset[0] = routing_start
        probs = at("probs", [P, GROUPS, E], F32, 4)
        key = at("key", [P, GROUPS, E], F32, 4)
        onehot = at("onehot", [P, GROUPS, TOPK, E], F32, 4)
        onehotb = at("onehotb", [P, GROUPS, TOPK * E], BF16, 2)
        earlier = at("earlier", [P, GROUPS, TOPK * E], BF16, 2)
        chosen = at("chosen", [P, GROUPS, TOPK * E], F32, 4)
        rank_of_e = at("rank_of_e", [P, E], F32, 4)
        first_slot = at("first_slot", [P, E], F32, 4)
        red = at("red", [P, GROUPS], F32, 4)
        rsum = at("rsum", [P, GROUPS], F32, 4)
        weight = at("weight", [P, GROUPS, TOPK], F32, 4)
        place = at("place", [P, GROUPS, TOPK], F32, 4)
        place0 = at("place0", [P, GROUPS, TOPK], F32, 4)
        keep = at("keep", [P, GROUPS, TOPK], F32, 4)
        slot_of = at("slot_of", [P, GROUPS, TOPK], I32, 4)
        entry = at("entry", [P, GROUPS, TOPK, 2], I32, 4)
        empty = at("empty", [P, E * CH, 2], I32, 4)
        zrows = at("zrows", [P, 2 * D], BF16, 2)

        attention_over = [s_pv.now(), s_ST.now(), s_x2t.now(), s_logit.now(), s_xt.now(), s_out.now(),
                          s_x2r.now(), s_ph.now(), s_pl.now(), s_mrowc.now(), s_gate.now()]
        attention_over += [s.now() for s in s_x1st + s_x2st + s_stack]
        pool.wait(*attention_over)
        s_iota = signal("s_iota")
        s_fill = dma_signal("s_fill")
        pool.do(gp.iota, rank_of_e[:, :], pattern=[[-1, E]], base=E, channel_multiplier=0,
                allow_small_or_imprecise_dtypes=True, done=s_iota)
        pool.do(gp.iota, first_slot[:, :], pattern=[[SLOTS, E]], base=0, channel_multiplier=0,
                allow_small_or_imprecise_dtypes=True, done=s_iota)
        pool.do(gp.memset, empty[:, :, 1], 0, done=s_iota)
        pool.do(gp.iota, empty[:, :, 0], pattern=[[0, E * CH]], base=T, channel_multiplier=1, done=s_iota)
        for k in range(TOPK):
            pool.do(gp.iota, entry[:, :, k, 0], pattern=[[P, GROUPS]], base=0, channel_multiplier=1, done=s_iota)
        pool.do(gp.memset, zrows[:, :], 0.0, done=s_iota)
        iotas = s_iota.now()
        sp.wait(iotas)
        sp.do(nc.sync.dma_start, table.rearrange("(e p c) two -> p e (c two)", p=P, c=CH),
              empty[:, :, :].rearrange("p (e c) two -> p e (c two)", e=E), done=s_fill)
        sp.do(nc.sync.dma_start, xn_rows[T:T + P, :], zrows[:, :], done=s_fill)
        sp.do(nc.sync.dma_start, out[T:T + P, :], zrows[:, :].bitcast(F32), done=s_fill)
        filled = s_fill.now()

        def wide(ap):
            return ap.unsqueeze(2).to_broadcast([P, GROUPS, E])

        def over_groups(ap):
            return ap.unsqueeze(1).to_broadcast([P, GROUPS, E])

        dve.wait(iotas, s_logit.now(), *attention_over)
        lg = logits[:, :, :]
        step(dv.tensor_reduce, red[:, :], lg, X_AXIS, ALU.max)
        m = step(dv.tensor_tensor, probs[:, :, :], lg, wide(red[:, :]), ALU.subtract)
        act.wait(m)
        m = act.do(ac.activation, probs[:, :, :], probs[:, :, :], ACT.Exp, done=s_act)
        dve.wait(m)
        step(dv.tensor_reduce, rsum[:, :], probs[:, :, :], X_AXIS, ALU.add)
        step(dv.reciprocal, rsum[:, :], rsum[:, :])
        step(dv.tensor_tensor, probs[:, :, :], probs[:, :, :], wide(rsum[:, :]), ALU.mult)
        for k in range(TOPK):
            step(dv.tensor_reduce, weight[:, :, k], probs[:, :, :], X_AXIS, ALU.max)
            step(dv.tensor_tensor, key[:, :, :], probs[:, :, :], wide(weight[:, :, k]), ALU.is_ge)
            step(dv.tensor_tensor, key[:, :, :], key[:, :, :], over_groups(rank_of_e[:, :]), ALU.mult)
            step(dv.tensor_reduce, red[:, :], key[:, :, :], X_AXIS, ALU.max)
            step(dv.tensor_tensor, onehot[:, :, k, :], over_groups(rank_of_e[:, :]), wide(red[:, :]), ALU.is_equal)
            if k == 0:
                step(dv.scalar_tensor_tensor, probs[:, :, :], onehot[:, :, 0, :], -2.0, probs[:, :, :], ALU.mult, ALU.add)
        step(dv.tensor_copy, onehotb[:, :, :], onehot[:, :, :, :].rearrange("p g k e -> p g (k e)"))
        step(dv.memset, earlier[:, 0, :], 0.0)
        for g in range(1, GROUPS):
            step(dv.tensor_tensor, earlier[:, g, :], earlier[:, g - 1, :], onehotb[:, g - 1, :], ALU.add)
        s_place = signal("s_place")
        pe.wait(s_dve.now(), bank_free[7])
        n_all = GROUPS * TOPK * E
        pe.do(mm, bank(7)[:, 0:n_all], before[:, :], onehotb[:, :, :].rearrange("p g k -> p (g k)"), start=True, stop=False)
        m = pe.do(mm, bank(7)[:, 0:n_all], ones[:, :], earlier[:, :, :].rearrange("p g k -> p (g k)"), start=False, stop=True, done=s_place)
        dve.wait(m)
        oh = onehot[:, :, :, :].rearrange("p g k e -> p (g k e)")
        ch = chosen[:, :, :].rearrange("p g k -> p (g k)")
        gk = GROUPS * TOPK
        step(dv.tensor_tensor, ch, bank(7)[:, 0:n_all], oh, ALU.mult)
        bank_free[7] = s_dve.now()
        step(dv.tensor_reduce, place[:, :, :].rearrange("p g k -> p (g k)"), ch.rearrange("p (a e) -> p a e", e=E), X_AXIS, ALU.add)
        step(dv.tensor_tensor, ch.rearrange("p (a e) -> p a e", e=E), oh.rearrange("p (a e) -> p a e", e=E),
             first_slot[:, :].unsqueeze(1).to_broadcast([P, gk, E]), ALU.mult)
        step(dv.tensor_reduce, place0[:, :, :].rearrange("p g k -> p (g k)"), ch.rearrange("p (a e) -> p a e", e=E), X_AXIS, ALU.add)
        step(dv.tensor_scalar, keep[:, :, :], place[:, :, :], float(CAP), float(DROPPED), ALU.is_ge, ALU.mult)
        step(dv.tensor_tensor, place[:, :, :], place[:, :, :], place0[:, :, :], ALU.add)
        step(dv.tensor_tensor, place[:, :, :], place[:, :, :], keep[:, :, :], ALU.add)
        step(dv.tensor_copy, slot_of[:, :, 0], place[:, :, 0])
        step(dv.tensor_scalar, slot_of[:, :, 1], place[:, :, 1], float(CAP), None, ALU.add)
        m = step(dv.tensor_copy, entry[:, :, :, 1].bitcast(F32), weight[:, :, :])
        s_scatter = dma_signal("s_scatter")
        pool.wait(m, iotas, filled)
        for g in range(GROUPS):
            for k in range(TOPK):
                pool.do(gp.indirect_dma_start, out=table, out_offset=bass.IndirectOffsetOnAxis(ap=slot_of[:, g, k:k + 1], axis=0),
                        in_=entry[:, g, k, :], in_offset=None, bounds_check=E * SLOTS - 1, oob_is_err=False, done=s_scatter)
        s_table = dma_signal("s_table")
        sp.wait(s_scatter.now())
        m_slots = sp.do(nc.sync.dma_start, slots[:, :, :, :].rearrange("p e c two -> p e (c two)"),
                        table.rearrange("(e p c) two -> p e (c two)", p=P, c=CH), done=s_table)

        s_gather = dma_signal("s_gather")
        s_et, s_etc_h, s_etc_l = signal("s_et"), signal("s_etc_h"), signal("s_etc_l")
        HALVES = [(0, CAP), (CAP, CAP)]
        E_UNITS, E_YBANKS, E_TR = [0, 2], [4, 5], [6, 7]
        attention_over += [s_up.now(), m_slots, s_dve.now()]
        rows_stored = [s.now() for s in s_x2st]
        for queue in (pe, act, dve, pool, sp):
            queue.wait(*attention_over)
        expert_x, et_read = {}, {}

        def gather(e):
            pool.wait(m_slots, filled, *rows_stored)
            if e:
                pool.wait(et_mark[e - 1])
            for c in range(CH):
                pool.do(gp.indirect_dma_start, out=xg[:, c, :], out_offset=None, in_=xn_rows,
                        in_offset=bass.IndirectOffsetOnAxis(ap=slots[:, e, c, 0:1], axis=0), bounds_check=T + P - 1,
                        oob_is_err=True, done=s_gather)
            gathered[e] = s_gather.now()

        gathered, et_mark = {}, {}

        def transpose_slots(e):
            pe.wait(gathered[e])
            if e >= 2:
                act.wait(et_read[e - 2])
                dve.wait(et_read[e - 2])
            for c in range(CH):
                b = E_TR[c % 2]
                pe.wait(bank_free[b])
                view = bank(b).bitcast(BF16)
                for j in range(2 * KB):
                    pe.do(tr, view[:, j * P:j * P + P], xg[:, c, j * P:j * P + P], identb[:, :], done=s_et if j == 2 * KB - 1 else None)
                m = s_et.now()
                dst = slice(c * P, c * P + P)
                src = view.rearrange("p (a k t) -> p a k t", a=2, k=KB)
                act.wait(m)
                mh = act.do(ac.activation, eth[e % 2][:, :, dst], src[:, 0], ACT.Copy, done=s_etc_h)
                act.wait(mh)
                ml = act.do(ac.activation, etl[e % 2][:, :, dst], src[:, 1], ACT.Copy, done=s_etc_l)
                bank_free[b] = ml
            et_mark[e] = s_et.now()
            expert_x[e] = [s_etc_h.now(), s_etc_l.now()]

        def store_expert(e, c):
            def store(n, b):
                y = yout[n % 3]
                act.wait(m_slots)
                m = act.do(ac.activation, y[:, :], bank(b), ACT.Copy, scale=slots[:, e, c, 1:2].bitcast(F32), done=s_y)
                pool.wait(m, filled, *[s.now() for s in s_yst])
                return m, pool.do(gp.indirect_dma_start, out=out, out_offset=bass.IndirectOffsetOnAxis(ap=slots[:, e, c, 0:1], axis=0),
                                  in_=y[:, :], in_offset=None, bounds_check=T + P - 1, oob_is_err=True, compute_op=ALU.add,
                                  done=s_yst[n % 3])
            return store

        gather(0)
        stage_free.clear()
        w1_ready["next"] = [w1_quarter([s[:, :] for s in stage], w1[0], q, s_up.now()) for q in range(4)]
        rank_down_weights(wd[0], s_up.now())
        transpose_slots(0)
        for e in range(E):
            w1_ready["now"] = w1_ready["next"]
            pe.wait(*expert_x[e])
            hi, lo = eth[e % 2], etl[e % 2]
            w2_free = last_down[0]
            r = rank_features(hi, lo, HALVES, E_UNITS)
            rank_up_weights(wu[e], e, w2_free)
            if e + 1 < E:
                gather(e + 1)
            first = count["up"]
            w2_ready["now"] = []
            for fb in range(FB):
                if fb % 4 == 0:
                    w2_ready["now"].append(w2_quarter([s[:, :] for s in stage], w2[e], fb // 4, w2_free))
                up_block(hi, lo, HALVES, fb, E_UNITS, b1cols[:, e * FB + fb:e * FB + fb + 1], hh, hl)
            et_read[e] = s_up.now()
            w1_free = s_up.now()
            w1_ready["next"] = []
            for c in range(CH):
                if c < 4 and e + 1 < E:
                    w1_ready["next"].append(w1_quarter([s[:, :] for s in stage], w1[e + 1], c, w1_free))
                for _ in down_chunk(c, first, r, E_YBANKS, store_expert(e, c), hh, hl):
                    pass
                if c == 1 and e + 1 < E:
                    rank_down_weights(wd[e + 1], w1_free)
                if c == 2 and e + 1 < E:
                    transpose_slots(e + 1)
            low_read[r] = last_down[0]
        sp.wait(*[s.now() for s in s_yst + s_x1st + s_x2st + [s_fill, s_scatter]])

        block = stack.enter_context(nc.Block())

        @block.sync
        def _(engine):
            sp.issue(engine)

        @block.gpsimd
        def _(engine):
            pool.issue(engine)

        @block.scalar
        def _(engine):
            act.issue(engine)

        @block.vector
        def _(engine):
            dve.issue(engine)

        @block.tensor
        def _(engine):
            pe.issue(engine)


_INPUTS = ["x", "ctx_2048", "itok_B_779_1933", "L0_ffn_gate_w", "L0_ffn_w1", "L0_ffn_b1", "L0_ffn_w2", "L0_ffn_b2",
           "L0_ffn_wd", "L0_ffn_wu", "L0_ffn_sw1", "L0_ffn_sb1", "L0_ffn_sw2", "L0_ffn_sb2", "L0_ffn_swd", "L0_ffn_swu"]


def kernel(**inputs):
    import concourse.bacc as bacc
    from concourse.bass_utils import run_bass_kernel_spmd

    nc = bacc.Bacc("TRN2", target_bir_lowering=False, num_devices=1, dynamic_dma_scratch_size=8192)
    arrays, args = {}, []
    for name in _INPUTS:
        a = np.ascontiguousarray(inputs[name])
        arrays[f"in_{name}"] = a
        args.append(nc.dram_tensor(f"in_{name}", a.shape, mybir.dt.from_np(a.dtype), kind="ExternalInput").ap())
    out = nc.dram_tensor("out_rows", (T + P, D), F32, kind="ExternalOutput").ap()
    build(nc, *args, out)
    r = run_bass_kernel_spmd(nc, [arrays], core_ids=[0])
    return r.results[0]["out_rows"][:T].reshape(B, C, L)
```

```python
from contextlib import ExitStack

import concourse.bass as bass
from concourse import mybir

import numpy as np

F32 = mybir.dt.float32
BF16 = mybir.dt.bfloat16
I32 = mybir.dt.int32
ALU = mybir.AluOpType
ACT = mybir.ActivationFunctionType
X_AXIS = mybir.AxisListType.X

P = 128
B, C, L = 8, 256, 512
T, D = B * C, L
HEADS, HD = 8, 32
GROUPS = T // P
GH = P // HD
QT = L // P
SCALE = 1.0 / (64 ** 0.5 * float(np.log(20)))
EPS = 1e-5
E, TOPK, RANK = 8, 2, 32
F = 4 * D
CAP = int(T * 1.25 / E)
SLOTS = TOPK * CAP
CH = SLOTS // P
KB, FB = D // P, F // P
PASS = 256
GPP = PASS // P
DROPPED = 1 << 14
WIDE = RANK * 3


class Signal:

    def __init__(self, sem, step):
        self.sem, self.step, self.value = sem, step, 0

    def now(self):
        return self, self.value


class Queue:

    def __init__(self):
        self.items, self.passed = [], {}

    def wait(self, *marks):
        for signal, value in marks:
            if self.passed.get(signal, 0) < value:
                self.passed[signal] = value
                self.items.append((None, signal.sem, value, None))

    def do(self, instruction, *args, done=None, **kwargs):
        self.items.append((instruction, args, kwargs, done))
        if done is not None:
            done.value += done.step
            return done.now()

    def issue(self, engine):
        for instruction, a, b, done in self.items:
            if instruction is None:
                engine.wait_ge(a, b)
            else:
                issued = instruction(*a, **b)
                if done is not None:
                    issued.then_inc(done.sem, done.step)


def build(nc, x, ctx_in, itok, gate_w, w1, b1, w2, b2, wd, wu, sw1, sb1, sw2, sb2, swd, swu, out):
    stack = ExitStack()
    with stack:
        def sb(name, shape, dt):
            return stack.enter_context(nc.sbuf_tensor(name, shape, dt))

        def signal(name, step=1):
            return Signal(stack.enter_context(nc.semaphore(name)), step)

        def dma_signal(name):
            return signal(name, 16)

        pe, act, dve, pool, sp = Queue(), Queue(), Queue(), Queue(), Queue()
        mm, tr = nc.tensor.matmul, nc.tensor.transpose
        dv, ac, gp = nc.vector, nc.scalar, nc.gpsimd

        x_rows = x.rearrange("b c l -> (b c) l")
        ctx_rows = ctx_in.rearrange("b c l -> (b c) l")
        xn_rows = nc.dram_tensor("normed_rows", [T + P, 2 * D], BF16, kind="Internal").ap()
        table = nc.dram_tensor("slot_table", [E * SLOTS, 2], I32, kind="Internal").ap()

        w1h, w1l = sb("w1h", [P, KB, F], BF16), sb("w1l", [P, KB, F], BF16)
        w2h, w2l = sb("w2h", [P, FB, D], BF16), sb("w2l", [P, FB, D], BF16)
        wdf = sb("wdf", [P, KB, RANK], F32)
        wdh, wdl = sb("wdh", [P, KB, WIDE], BF16), sb("wdl", [P, KB, WIDE], BF16)
        wuf, wus = sb("wuf", [WIDE, D], F32), sb("wus", [P, D], BF16)
        hidden = sb("hidden", [P, 2 * FB * SLOTS], BF16)
        hh, hl = (hidden[:, k * FB * SLOTS:(k + 1) * FB * SLOTS].rearrange("p (f n) -> p f n", n=SLOTS) for k in range(2))
        hf = [sb(f"hf{i}", [P, SLOTS], F32) for i in range(2)]
        low = [sb(f"low{i}", [P, SLOTS], BF16) for i in range(2)]
        lowf = sb("lowf", [WIDE, SLOTS], F32)
        yout = [sb(f"yout{i}", [P, D], F32) for i in range(3)]
        ident = sb("ident", [P, P], F32)
        identb = sb("identb", [P, P], BF16)
        before = sb("before", [P, P], BF16)
        ones = sb("ones", [P, P], BF16)
        half = sb("half", [P, 1], F32)
        b1rows, b1cols = sb("b1rows", [P, P], F32), sb("b1cols", [P, E * FB], F32)
        sb1rows, sb1cols = sb("sb1rows", [FB, P], F32), sb("sb1cols", [P, FB], F32)
        b2f = sb("b2f", [E + 1, D], F32)
        b2parts = sb("b2parts", [E + 1, 3, D], BF16)
        gate = sb("gate", [P, KB, E], F32)
        logits = sb("logits", [P, GROUPS, E], F32)
        slots = sb("slots", [P, E, CH, 2], I32)

        base = nc.sbuf_base
        offset = [base + (-base) % 64]
        region_start = offset[0]
        limit = nc.sbuf_usable_end

        def at(name, shape, dt, size):
            n = size
            for s in shape[1:]:
                n *= s
            t = nc.alloc_sbuf_tensor_at(name, shape, dt, offset=offset[0])
            offset[0] += n + (-n) % 64
            if offset[0] > limit:
                raise ValueError(f"{name} ends at {offset[0]}, {limit} is the limit")
            return t

        xth = [at(f"xth{i}", [P, KB, PASS], BF16, 2) for i in range(2)]
        xtl = [at(f"xtl{i}", [P, KB, PASS], BF16, 2) for i in range(2)]
        NX, NS = 4, 4
        xin = [at(f"xin{i}", [P, L], F32, 4) for i in range(NX)]
        cin = [at(f"cin{i}", [P, L], F32, 4) for i in range(2)]
        xn = at("xn", [P, L], F32, 4)
        routing_start = offset[0]
        QS = [at(f"QS{i}", [P, GH, L], BF16, 2) for i in range(NS)]
        KS = [at(f"KS{i}", [P, GH, L], BF16, 2) for i in range(NS)]
        VT = [at(f"VT{i}", [P, 2, QT, P], BF16, 2) for i in range(2)]
        prob = [at(f"prob{i}", [P, L], F32, 4) for i in range(3)]
        shh, shl = (hidden[:, k * FB * PASS:(k + 1) * FB * PASS].rearrange("p (f n) -> p f n", n=PASS) for k in range(2))
        NPH = 8
        spare = hidden[:, 2 * FB * PASS:2 * FB * PASS + 2 * NPH * L].rearrange("p (n l) -> p n l", l=L)
        ph = [spare[:, i, :] for i in range(NPH)]
        pl = [spare[:, NPH + i, :] for i in range(NPH)]
        split = [hidden[:, 2 * FB * PASS + (2 * NPH + 4 * i) * L:][:, 0:4 * L].rearrange("p (n l) -> p n l", l=L) for i in range(2)]
        rowmax = [at(f"rowmax{i}", [P, GH * QT], F32, 4) for i in range(2)]
        MS = at("MS", [P, GH * QT, HD], BF16, 2)
        rden = at("rden", [P, L], F32, 4)
        x2s = [at(f"x2_{i}", [P, L], F32, 4) for i in range(2)]
        x2r = [at(f"x2r{i}", [P, 2, L], BF16, 2) for i in range(2)]
        x2t = at("x2t", [P, KB, P], F32, 4)
        stat = at("stat", [P, 2, 6], F32, 4)
        mv = at("mv", [P, 2, 4], F32, 4)
        scale_i = at("scale_i", [P, B], I32, 4)
        scale_f = at("scale_f", [P, B], F32, 4)
        scales = at("scales", [P, B], F32, 4)

        offset[0] = region_start
        NST = 3
        stage = [at(f"stage{i}", [P, 2048], F32, 4) for i in range(NST)]
        xg = at("xg", [P, CH, 2 * D], BF16, 2)
        eth = [at(f"eth{i}", [P, KB, SLOTS], BF16, 2) for i in range(2)]
        etl = [at(f"etl{i}", [P, KB, SLOTS], BF16, 2) for i in range(2)]
        PB = stack.enter_context(nc.psum_tensor("banks", [P, 8, 512], F32))

        def bank(i):
            return PB[:, i, :]

        s_const = signal("s_const")
        s_pool = signal("s_pool")
        s_dve = signal("s_dve")
        s_act = signal("s_act")
        s_small = dma_signal("s_small")

        def fill(view, value):
            pool.do(gp.memset, view, value, done=s_pool)
            pool.wait(s_pool.now())

        small = []
        small.append(sp.do(nc.sync.dma_start, scale_i[:, :], itok.rearrange("(a b) -> a b", a=1).partition_broadcast(P).rearrange("p a b -> p (a b)"), done=s_small))
        small.append(sp.do(nc.sync.dma_start, gate[:, :, :], gate_w.rearrange("(k p) e -> p k e", p=P), done=s_small))
        small.append(sp.do(nc.sync.dma_start, b1rows[:, :], b1.rearrange("e (c p) -> (e c) p", p=P), done=s_small))
        small.append(sp.do(nc.sync.dma_start, sb1rows[:, :], sb1.rearrange("(c p) -> c p", p=P), done=s_small))
        small.append(sp.do(nc.sync.dma_start, b2f[0:E, :], b2, done=s_small))
        small.append(sp.do(nc.sync.dma_start, b2f[E:E + 1, :], sb2.rearrange("(a d) -> a d", a=1), done=s_small))
        loaded_small = small[-1]

        fill(ident[:, :], 0.0)
        pool.do(gp.affine_select, out=ident[:, :], in_=ident[:, :], compare_op=ALU.not_equal, fill=1.0,
                base=0, pattern=[[-1, P]], channel_multiplier=1, done=s_pool)
        pool.wait(s_pool.now())
        pool.do(gp.tensor_copy, identb[:, :], ident[:, :], done=s_const)
        fill(before[:, :], 0.0)
        pool.do(gp.affine_select, out=before[:, :], in_=before[:, :], compare_op=ALU.is_ge, fill=1.0,
                base=0, pattern=[[-1, P]], channel_multiplier=1, done=s_const)
        pool.wait(s_const.now())
        fill(ones[:, :], 1.0)
        fill(half[:, :], -0.5)
        fill(MS[:, :, :], 0.0)
        fill(wus[96:P, :], 0.0)
        for i in range(2):
            fill(low[i][96:P, :], 1.0)
        for i in range(NS):
            fill(KS[i][96:P, :, :], 1.0)
        constants = s_pool.now()
        for queue in (dve, pe, act):
            queue.wait(s_const.now(), constants)

        s_scale = signal("s_scale")
        dve.wait(loaded_small)
        m = dve.do(dv.tensor_copy, scale_f[:, :], scale_i[:, :], done=s_dve)
        act.wait(m)
        m = act.do(ac.activation, scales[:, :], scale_f[:, :], ACT.Ln, done=s_act)
        dve.wait(m)
        m_scale = dve.do(dv.tensor_scalar, scales[:, :], scales[:, :], SCALE, None, ALU.mult, done=s_scale)
        act.wait(m_scale)
        def step(*args, **kwargs):
            mark = dve.do(*args, done=s_dve, **kwargs)
            dve.wait(mark)
            return mark

        def chain():
            last = []

            def link(*args, done=s_dve, **kwargs):
                dve.wait(*last)
                last[:] = [dve.do(*args, done=done, **kwargs)]
                return last[0]
            return link

        step(dv.tensor_copy, b2parts[:, 0, :], b2f[:, :])
        step(dv.tensor_tensor, b2f[:, :], b2f[:, :], b2parts[:, 0, :], ALU.subtract)
        step(dv.tensor_copy, b2parts[:, 1, :], b2f[:, :])
        m_b2 = step(dv.tensor_tensor, b2parts[:, 2, :], b2f[:, :], b2parts[:, 1, :], ALU.subtract)
        s_bias = signal("s_bias")
        s_biasc = signal("s_biasc")
        pe.wait(loaded_small)
        pe.do(tr, bank(3)[:, 0:P], b1rows[:, :], ident[:, :])
        m = pe.do(tr, bank(3)[:, P:P + FB], sb1rows[:, :], ident[0:FB, 0:FB], done=s_bias)
        dve.wait(m)
        dve.do(dv.tensor_copy, b1cols[:, :], bank(3)[:, 0:P], done=s_biasc)
        m_biascols = dve.do(dv.tensor_copy, sb1cols[:, :], bank(3)[:, P:P + FB], done=s_biasc)
        act.wait(m_biascols)

        s_x = [dma_signal(f"s_x{i}") for i in range(NX)]
        s_c = [dma_signal(f"s_c{i}") for i in range(2)]
        s_rstd = signal("s_rstd")
        s_split = signal("s_split")
        s_khi = signal("s_khi")
        s_stack = [dma_signal(f"s_stack{i}") for i in range(NS)]
        s_vt, s_vtc = signal("s_vt"), signal("s_vtc")
        s_phv = signal("s_phv")
        s_S, s_max = signal("s_S"), signal("s_max")
        s_ms, s_mrow, s_mrowc = signal("s_ms"), signal("s_mrow"), signal("s_mrowc")
        s_ST, s_exp, s_ph, s_pl, s_pv = (signal(n) for n in ("s_ST", "s_exp", "s_ph", "s_pl", "s_pv"))
        s_out = signal("s_out")
        s_x1st = [dma_signal(f"s_x1st{i}") for i in range(GROUPS)]
        s_x2, s_x2r = signal("s_x2hi"), signal("s_x2lo")
        s_x2st = [dma_signal(f"s_x2st{i}") for i in range(2)]
        s_x2t, s_x2tc = signal("s_x2t"), signal("s_x2tc")
        s_gate, s_logit, s_xt = signal("s_gate"), signal("s_logit"), signal("s_xt")

        x_loaded, c_loaded, split_done, khi_done, stacked, vt_done = {}, {}, {}, {}, {}, {}
        s_released, st_done, mrow_done, out_done, x1_stored, x2_stored = {}, {}, {}, {}, {}, {}
        xt_ready = {}
        bank_free = {i: m_biascols for i in range(8)}

        def layer_norm(src, dst, k, link):
            link(dv.bn_stats, stat[:, k, :], src)
            yield
            link(dv.bn_aggr, mv[:, k, 0:2], stat[:, k, :])
            yield
            m = link(dv.tensor_scalar, mv[:, k, 2:3], mv[:, k, 1:2], EPS, None, ALU.add)
            pool.wait(m)
            m = pool.do(gp.tensor_tensor, mv[:, k, 3:4], mv[:, k, 2:3], half[:, :], ALU.pow, done=s_rstd)
            yield
            yield
            dve.wait(m)
            link(dv.tensor_scalar, dst, src, mv[:, k, 0:1], mv[:, k, 3:4], ALU.subtract, ALU.mult)
            yield

        def load_group(g):
            rows = slice(P * g, P * g + P)
            if g >= NX:
                sp.wait(x2_done[g - NX], x1_stored[g - NX])
            x_loaded[g] = sp.do(nc.sync.dma_start, xin[g % NX][:, :], x_rows[rows, :], done=s_x[g % NX])
            if g >= 2:
                sp.wait(split_done[g - 2], khi_done[g - 2])
            c_loaded[g] = sp.do(nc.sync.dma_start, cin[g % 2][:, :], ctx_rows[rows, :], done=s_c[g % 2])

        def prepare(g):
            s, part = g % NS, split[g % 2]
            if g >= 2:
                dve.wait(stacked[g - 2])
                act.wait(stacked[g - 2])
                act.wait(vt_done[g - 2])
                dve.wait(vt_done[g - 2])
            link = chain()
            dve.wait(x_loaded[g])
            if g:
                dve.wait(split_done[g - 1])
            yield from layer_norm(xin[g % NX][:, :], xn[:, :], 0, link)
            link(dv.tensor_copy, part[:, 0, :], xn[:, :])
            act.wait(c_loaded[g])
            khi_done[g] = act.do(ac.activation, part[:, 2, :], cin[g % 2][:, :], ACT.Copy, done=s_khi)
            yield
            link(dv.tensor_tensor, part[:, 1, :], xn[:, :], part[:, 0, :], ALU.subtract, done=s_split)
            yield
            dve.wait(khi_done[g], c_loaded[g])
            split_done[g] = dve.do(dv.tensor_tensor, part[:, 3, :], cin[g % 2][:, :], part[:, 2, :],
                                   ALU.subtract, done=s_split)
            yield
            if g >= NS:
                sp.wait(st_done[g - NS])
            sp.wait(split_done[g], khi_done[g])
            for dst, parts in ((QS[s], (0, 1, 0)), (KS[s], (2, 2, 3))):
                for k, which in enumerate(parts):
                    for h in range(GH):
                        rows = slice(HD * h, HD * h + HD)
                        sp.do(nc.sync.dma_start, dst[HD * k:HD * k + HD, h, :], part[rows, which, :], done=s_stack[s])
            stacked[g] = s_stack[s].now()
            yield

        def transpose_values(g, b):
            pe.wait(split_done[g], khi_done[g], bank_free[b])
            view = bank(b).bitcast(BF16)
            for k in range(2):
                for t in range(QT):
                    at_ = (k * QT + t) * P
                    pe.do(tr, view[:, at_:at_ + P], split[g % 2][:, 2 + k, t * P:t * P + P], identb[:, :],
                          done=s_vt if (k, t) == (1, QT - 1) else None)
            vt_done[g] = s_vt.now()
            act.wait(vt_done[g])
            if g >= 2:
                act.wait(pv_done[g - 2])
            bank_free[b] = act.do(ac.activation, VT[g % 2][:, :, :, :].rearrange("p a t c -> p (a t c)"), view[:, :],
                                  ACT.Copy, done=s_vtc)
            vtc_done[g] = bank_free[b]

        pv_done, vtc_done = {}, {}

        def score_max(g, i, b):
            h, t = divmod(i, QT)
            s = g % NS
            pe.wait(stacked[g], bank_free[b])
            m = pe.do(mm, bank(b), QS[s][0:96, h, t * P:t * P + P], KS[s][0:96, h, :], start=True, stop=True, done=s_S)
            dve.wait(m)
            bank_free[b] = dve.do(dv.reduce_max, rowmax[g % 2][:, i:i + 1], bank(b), X_AXIS, done=s_max)

        def max_rows(g, b):
            s = g % NS
            dve.wait(s_max.now())
            if g:
                dve.wait(mrow_done[g - 1])
            mx = rowmax[g % 2][:, :]
            step(dv.tensor_scalar, MS[:, :, 0], mx, -1.0, None, ALU.mult)
            m = dve.do(dv.scalar_tensor_tensor, MS[:, :, 1], mx, -1.0, MS[:, :, 0], ALU.mult, ALU.subtract, done=s_ms)
            pe.wait(m, bank_free[b])
            for t in range(QT):
                for h in range(GH):
                    last = (t, h) == (QT - 1, GH - 1)
                    pe.do(mm, bank(b)[HD * h:HD * h + HD, t * P:t * P + P], MS[:, h * QT + t, :], identb[:, :],
                          start=True, stop=True, done=s_mrow if last else None)
            mrow_done[g] = s_mrow.now()
            act.wait(mrow_done[g])
            for h in range(GH):
                act.do(ac.activation, QS[s][96:P, h, :], bank(b)[HD * h:HD * h + HD, :], ACT.Copy, done=s_mrowc)
            bank_free[b] = s_mrowc.now()
            mrowc_done[g] = bank_free[b]

        mrowc_done = {}
        tick = {"st": 0}
        ph_mark, pl_mark, ph_read = {}, {}, {}

        def exponentials(g, i, b):
            t, h = divmod(i, GH)
            s, n = g % NS, tick["st"]
            tick["st"] += 1
            pe.wait(stacked[g], mrowc_done[g], bank_free[b])
            m = pe.do(mm, bank(b), KS[s][:, h, t * P:t * P + P], QS[s][:, h, :], start=True, stop=True, done=s_ST)
            act.wait(m)
            if n >= 3:
                act.wait(ph_mark[n - 3], pl_mark[n - 3])
            m = act.do(ac.activation, prob[n % 3][:, :], bank(b), ACT.Exp, scale=scales[:, g // 2:g // 2 + 1], done=s_exp)
            bank_free[b] = m
            if n >= NPH:
                (dve if n % 2 else act).wait(ph_read[n - NPH])
                pool.wait(ph_read[n - NPH])
            if n % 2:
                dve.wait(m)
                ph_mark[n] = dve.do(dv.tensor_copy, ph[n % NPH], prob[n % 3][:, :], done=s_phv)
            else:
                act.wait(m)
                ph_mark[n] = act.do(ac.activation, ph[n % NPH], prob[n % 3][:, :], ACT.Copy, done=s_ph)
            pool.wait(ph_mark[n], m)
            pl_mark[n] = pool.do(gp.tensor_tensor, pl[n % NPH], prob[n % 3][:, :], ph[n % NPH],
                                 ALU.subtract, done=s_pl)
            if i == GH * QT - 1:
                st_done[g] = s_ST.now()

        def weighted_values(g, t, b_out, b_sum):
            n0 = g * GH * QT + t * GH
            v = VT[g % 2]
            pe.wait(vtc_done[g], ph_mark[n0 + GH - 2], ph_mark[n0 + GH - 1], pl_mark[n0 + GH - 1])
            if t == 0:
                pe.wait(bank_free[b_out], bank_free[b_sum])
            work = [(b_sum, None, ph), (b_out, 0, ph), (b_out, 1, ph), (b_sum, None, pl), (b_out, 0, pl)]
            opened = set()
            for k, (b, part, src) in enumerate(work):
                for h in range(GH):
                    cols = slice(HD * h, HD * h + HD)
                    lhsT = ones[:, 0:HD] if part is None else v[:, part, t, cols]
                    last = (k, h) == (len(work) - 1, GH - 1)
                    pe.do(mm, bank(b)[cols, :], lhsT, src[(n0 + h) % NPH],
                          start=t == 0 and b not in opened, stop=t == QT - 1 and k >= 3, done=s_pv if last else None)
                opened.add(b)
            for h in range(GH):
                ph_read[n0 + h] = s_pv.now()
            if t == QT - 1:
                pv_done[g] = s_pv.now()

        def finish_attention(g, b_out, b_sum):
            rows = slice(P * g, P * g + P)
            link = chain()
            dve.wait(pv_done[g])
            if g:
                dve.wait(out_done[g - 1])
            for q in range(QT):
                cols = slice(q * P, q * P + P)
                link(dv.reciprocal, rden[:, cols], bank(b_sum)[:, cols])
                yield
            bank_free[b_sum] = s_dve.now()
            o = xin[g % NX]
            bank_free[b_out] = link(dv.tensor_tensor, rden[:, :], bank(b_out), rden[:, :], ALU.mult)
            yield
            out_done[g] = link(dv.tensor_tensor, o[:, :], o[:, :], rden[:, :], ALU.add, done=s_out)
            sp.wait(out_done[g])
            x1_stored[g] = sp.do(nc.sync.dma_start, out[rows, :], o[:, :], done=s_x1st[g])
            yield
            x2 = x2s[g % 2]
            if g >= 2:
                dve.wait(x2t_done[g - 2])
            yield from layer_norm(o[:, :], x2[:, :], 1, link)
            x2_done[g] = s_dve.now()
            if g >= 2:
                dve.wait(x2_stored[g - 2])
            r = x2r[g % 2]
            link(dv.tensor_copy, r[:, 0, :], x2[:, :])
            yield
            m = link(dv.tensor_tensor, r[:, 1, :], x2[:, :], r[:, 0, :], ALU.subtract, done=s_x2r)
            sp.wait(m)
            x2_stored[g] = sp.do(nc.sync.dma_start, xn_rows[rows, :], r[:, :, :].rearrange("p a d -> p (a d)"), done=s_x2st[g % 2])
            yield

        x2t_done, x2_done = {}, {}

        def transpose_tokens(g, b):
            p, col = g // GPP, (g % GPP) * P
            x2 = x2s[g % 2]
            pe.wait(x2_done[g], bank_free[b])
            for k in range(KB):
                pe.do(tr, bank(b)[:, k * P:k * P + P], x2[:, k * P:k * P + P], ident[:, :], done=s_x2t if k == KB - 1 else None)
            x2t_done[g] = s_x2t.now()
            act.wait(x2t_done[g])
            if g:
                act.wait(xt_ready[g - 1], gate_done[g - 1])
            m = act.do(ac.activation, x2t[:, :, :].rearrange("p k t -> p (k t)"), bank(b), ACT.Copy, done=s_x2tc)
            pe.wait(m)
            for k in range(KB):
                pe.do(mm, bank(b)[:, 0:E], x2t[:, k, :], gate[:, k, :], start=k == 0, stop=k == KB - 1,
                      done=s_gate if k == KB - 1 else None)
            gate_done[g] = s_gate.now()
            hi, lo = xth[p % 2][:, :, col:col + P], xtl[p % 2][:, :, col:col + P]
            dve.wait(m)
            if p >= 2:
                dve.wait(pass_up_done[p - 2])
            step(dv.tensor_copy, hi, x2t[:, :, :])
            xt_ready[g] = dve.do(dv.tensor_tensor, lo, x2t[:, :, :], hi, ALU.subtract, done=s_xt)
            dve.wait(gate_done[g])
            bank_free[b] = dve.do(dv.tensor_copy, logits[:, g, :], bank(b)[:, 0:E], done=s_logit)

        gate_done, pass_up_done = {}, {}

        s_up, s_gelu, s_hh, s_hl = signal("s_up"), signal("s_gelu"), signal("s_hh"), signal("s_hl")
        s_hha, s_hlp = signal("s_hha"), signal("s_hlp")
        s_down, s_y = signal("s_down"), signal("s_y")
        s_yst = [dma_signal(f"s_yst{i}") for i in range(3)]
        count = {"up": 0, "down": 0, "rank": 0}
        gelu_mark, h_split, low_done, y_stored = {}, {}, {}, {}
        low_read = {}
        last_down = [constants]
        w1_ready, w2_ready, wd_ready, wu_ready = {}, {}, {}, {}

        def rank_features(x_hi, x_lo, halves, units):
            n = count["rank"]
            count["rank"] += 1
            b0 = units[count["up"] % len(units)]
            count["up"] += 1
            pe.wait(wd_ready["now"], *[bank_free[b0 + j] for j in range(len(halves))])
            for j, (c0, w) in enumerate(halves):
                k = 0
                for weights, data in ((wdh, x_hi), (wdh, x_lo), (wdl, x_hi)):
                    for kb in range(KB):
                        k += 1
                        pe.do(mm, bank(b0 + j)[0:WIDE, 0:w], weights[:, kb, :], data[:, kb, c0:c0 + w],
                              start=k == 1, stop=k == 3 * KB, done=s_up if (j, k) == (len(halves) - 1, 3 * KB) else None)
            act.wait(s_up.now())
            w, total = halves[0][1], sum(w for _, w in halves)
            if n:
                act.wait(low_done[n - 1])
            m = act.do(ac.activation, lowf[:, 0:total].rearrange("p (j w) -> p j w", w=w), PB[0:WIDE, b0:b0 + len(halves), 0:w],
                       ACT.Gelu, done=s_gelu)
            for j in range(len(halves)):
                bank_free[b0 + j] = m
            o = low[n % 2]
            dve.wait(m)
            if n >= 2:
                dve.wait(low_read[n - 2])
            step(dv.tensor_copy, o[0:WIDE, 0:total], lowf[:, 0:total])
            low_done[n] = step(dv.tensor_tensor, o[HD:2 * HD, 0:total], lowf[HD:2 * HD, 0:total], o[HD:2 * HD, 0:total], ALU.subtract)
            return n

        def up_block(x_hi, x_lo, halves, fb, units, bias, hh, hl, shared=False):
            n = count["up"]
            count["up"] += 1
            b0 = units[n % len(units)]
            pe.wait(w1_ready["now"][fb // 4], *[bank_free[b0 + j] for j in range(len(halves))])
            f0 = fb * P
            k = 0
            for weights, data in ((w1h, x_hi), (w1h, x_lo), (w1l, x_hi)):
                for kb in range(KB):
                    k += 1
                    for j, (c0, w) in enumerate(halves):
                        pe.do(mm, bank(b0 + j)[:, 0:w], weights[:, kb, f0:f0 + P], data[:, kb, c0:c0 + w],
                              start=k == 1, stop=k == 3 * KB, done=s_up if (j, k) == (len(halves) - 1, 3 * KB) else None)
            act.wait(s_up.now())
            w, total = halves[0][1], sum(w for _, w in halves)
            ring = 4 if total <= SLOTS // 2 else 2
            if n - ring in h_split:
                act.wait(h_split[n - ring])
            h_out = hf[n % 2][:, (n % ring) // 2 * total:][:, 0:total]
            m = act.do(ac.activation, h_out.rearrange("p (j w) -> p j w", w=w),
                       PB[:, b0:b0 + len(halves), 0:w], ACT.Gelu, bias=bias, done=s_gelu)
            for j in range(len(halves)):
                bank_free[b0 + j] = m
            if shared:
                act.wait(m, last_down[0])
                m = act.do(ac.activation, hh[:, fb, 0:total], h_out, ACT.Copy, done=s_hha)
                pool.wait(m, last_down[0])
                h_split[n] = pool.do(gp.tensor_tensor, hl[:, fb, 0:total], h_out, hh[:, fb, 0:total],
                                     ALU.subtract, done=s_hlp)
            else:
                dve.wait(m, last_down[0])
                dve.wait(dve.do(dv.tensor_copy, hh[:, fb, 0:total], h_out, done=s_hh))
                h_split[n] = dve.do(dv.tensor_tensor, hl[:, fb, 0:total], h_out, hh[:, fb, 0:total],
                                    ALU.subtract, done=s_hl)
            return n

        def down_chunk(c, first_up, rank_n, ybanks, store, hh, hl):
            n = count["down"]
            count["down"] += 1
            b = ybanks[n % len(ybanks)]
            cols = slice(c * P, c * P + P)
            pe.wait(bank_free[b], low_done[rank_n], wu_ready["now"])
            pe.do(mm, bank(b), low[rank_n % 2][:, cols], wus[:, :], start=True, stop=False)
            for fb in range(FB):
                pe.wait(h_split[first_up + fb], w2_ready["now"][fb // 4])
                for k, (a, w) in enumerate(((hh, w2h), (hh, w2l), (hl, w2h))):
                    last = (fb, k) == (FB - 1, 2)
                    pe.do(mm, bank(b), a[:, fb, cols], w[:, fb, :], start=False, stop=last, done=s_down if last else None)
                yield
            last_down[0] = down = s_down.now()
            yield
            act.wait(down)
            if n >= 3:
                act.wait(y_stored[n - 3])
            bank_free[b], y_stored[n] = store(n, b)

        s_stage = [dma_signal(f"s_stage{i}") for i in range(NST)]
        s_wd, s_wu = dma_signal("s_wd"), dma_signal("s_wu")
        s_rankb = dma_signal("s_rankb")
        s_whi, s_wlo = signal("s_whi"), signal("s_wlo")
        count["stage"] = 0
        stage_free = {}

        def load_weights(stages, src, dst_hi, dst_lo, written_over):
            n = count["stage"]
            count["stage"] += 1
            i = n % len(stages)
            sp.wait(*stage_free.get(i, []))
            a, w = src.shape[1], src.shape[2]
            buf = stages[i].rearrange("p (a w) -> p a w", w=w)
            m = sp.do(nc.sync.dma_start, buf, src, done=s_stage[i])

            def split_them():
                act.wait(m, *written_over)
                hi = act.do(ac.activation, dst_hi, buf, ACT.Copy, done=s_whi)
                dve.wait(m, hi, *written_over)
                lo = dve.do(dv.tensor_tensor, dst_lo, buf, dst_hi, ALU.subtract, done=s_wlo)
                stage_free[i] = [hi, lo]
                return lo
            return split_them

        def w1_quarter(stages, w, q, written_over):
            cols = slice(q * 512, q * 512 + 512)
            return load_weights(stages, w.rearrange("(k p) f -> p k f", p=P)[:, :, cols], w1h[:, :, cols], w1l[:, :, cols], written_over)

        def w2_quarter(stages, w, q, written_over):
            rows = slice(q * 4, q * 4 + 4)
            return load_weights(stages, w.rearrange("(k p) d -> p k d", p=P)[:, rows, :], w2h[:, rows, :], w2l[:, rows, :], written_over)

        def rank_down_weights(w, written_over):
            sp.wait(written_over, *stage_free.get("wd", []))
            m = sp.do(nc.sync.dma_start, wdf[:, :, :], w.rearrange("(k p) r -> p k r", p=P), done=s_wd)
            dve.wait(m, written_over)
            for j in range(3):
                step(dv.tensor_copy, wdh[:, :, j * RANK:(j + 1) * RANK], wdf[:, :, :])
            for j in range(3):
                step(dv.tensor_tensor, wdl[:, :, j * RANK:(j + 1) * RANK], wdf[:, :, :], wdh[:, :, j * RANK:(j + 1) * RANK], ALU.subtract)
            stage_free["wd"] = [s_dve.now()]
            wd_ready["now"] = s_dve.now()

        def rank_up_weights(w, bias_row, written_over):
            sp.wait(written_over, m_b2, *stage_free.get("wu", []))
            for j in range(3):
                sp.do(nc.sync.dma_start, wuf[j * RANK:(j + 1) * RANK, :], w, done=s_wu)
            wu_loaded = s_wu.now()
            for j in range(3):
                sp.do(nc.sync.dma_start, wus[96 + j:97 + j, :], b2parts[bias_row:bias_row + 1, j, :], done=s_rankb)
            dve.wait(wu_loaded, written_over)
            step(dv.tensor_copy, wus[0:WIDE, :], wuf[:, :])
            m = step(dv.tensor_tensor, wus[64:96, :], wuf[64:96, :], wus[64:96, :], ALU.subtract)
            stage_free["wu"] = [m]
            dve.wait(s_rankb.now())
            wu_ready["now"] = m
            pe.wait(s_rankb.now())

        hstage = [hidden[:, k * FB * PASS:(k + 1) * FB * PASS].bitcast(F32) for k in range(2)]

        def shared_weights():
            w1_ready["now"], w2_ready["now"] = [], []
            quarters = [(w1_quarter, sw1, q, w1_ready) for q in range(4)] + [(w2_quarter, sw2, q, w2_ready) for q in range(4)]
            loads = [f(hstage, w, q, [constants]) for f, w, q, _ in quarters[:2]]
            yield
            for k, quarter in enumerate(quarters):
                quarter[3]["now"].append(loads[k]())
                if k + 2 < len(quarters):
                    f, w, q, _ = quarters[k + 2]
                    loads.append(f(hstage, w, q, [constants]))
                yield
            rank_down_weights(swd, constants)
            rank_up_weights(swu, E, constants)
            yield

        added = {}

        def store_shared(p, c):
            def store(n, b):
                y = yout[n % 3]
                m = act.do(ac.activation, y[:, :], bank(b), ACT.Copy, scale=0.2, done=s_y)
                rows = slice((p * GPP + c) * P, (p * GPP + c) * P + P)
                pool.wait(m, x1_stored[p * GPP + c])
                return m, pool.do(gp.dma_start, out[rows, :], y[:, :], accum_op=ALU.add, done=s_yst[n % 3])
            return store

        FFN_BANKS = [6, 7]
        pass_state = {}

        def shared_up(p):
            hi, lo = xth[p % 2], xtl[p % 2]
            pe.wait(*[xt_ready[p * GPP + i] for i in range(GPP)])
            halves = [(0, PASS)]
            r = rank_features(hi, lo, halves, FFN_BANKS)
            pass_state[p] = (count["up"], r)
            yield
            for fb in range(FB):
                up_block(hi, lo, halves, fb, FFN_BANKS, sb1cols[:, fb:fb + 1], shh, shl, shared=True)
                yield
            pass_up_done[p] = s_up.now()

        def shared_down(p):
            first, r = pass_state[p]
            for c in range(GPP):
                yield from down_chunk(c, first, r, FFN_BANKS, store_shared(p, c), shh, shl)
            low_read[r] = last_down[0]

        def without_exponentials(w):
            side = finish_attention(2 * w - 1, *PV_BANKS[1]) if w >= 1 else iter(())
            for k, g in enumerate((2 * w, 2 * w + 1)):
                if g < GROUPS:
                    transpose_values(g, 3 if k else 6)
                for i in range(GH * QT):
                    if g < GROUPS:
                        score_max(g, i, i % 2)
                    next(side, None)
                    if k == 0 and i == 15:
                        for _ in side:
                            pass
                        for n in (2 * w + 2, 2 * w + 3):
                            if n < GROUPS:
                                load_group(n)
                    if (k, i) in ((0, 4), (1, 4)) and w >= 1:
                        transpose_tokens(g - 2, 2 if k else 7)
                    if i % 2:
                        yield
                if g < GROUPS:
                    max_rows(g, 3)

        def with_exponentials(w):
            for k, g in enumerate((2 * w, 2 * w + 1)):
                side = []
                if k == 1:
                    side.append(finish_attention(g - 1, *PV_BANKS[0]))
                if g + 2 < GROUPS:
                    side.append(prepare(g + 2))
                for i in range(GH * QT):
                    exponentials(g, i, i % 2)
                    if i % GH == GH - 1 and i >= 2 * GH - 1:
                        weighted_values(g, i // GH - 1, *PV_BANKS[k])
                    if i >= 1:
                        for _ in range(1 + k):
                            while side and next(side[0], "over") == "over":
                                side.pop(0)
                    if i % 4 == 3:
                        next(weights, None)
                    yield
                for rest in side:
                    for _ in rest:
                        pass
                weighted_values(g, QT - 1, *PV_BANKS[k])

        def together(main, other, ratio):
            owed = 0.0
            for _ in main:
                owed += ratio
                while owed >= 1:
                    owed -= 1
                    next(other, None)
            for _ in other:
                pass

        PV_BANKS = [(4, 5), (2, 3)]
        weights = shared_weights()
        load_group(0)
        load_group(1)
        for g in range(2):
            for _ in prepare(g):
                pass
        next(weights)
        LAST = GROUPS // 2
        for w in range(LAST + 2):
            p = w - 2
            up = shared_up(p) if p >= 0 else iter(())
            down = shared_down(p) if p >= 0 else iter(())
            if p == 0:
                for _ in weights:
                    pass
            together(without_exponentials(w) if w <= LAST else iter(()), up, 17 / 16)
            together(with_exponentials(w) if w < LAST else iter(()), down, 1)

        offset[0] = routing_start
        probs = at("probs", [P, GROUPS, E], F32, 4)
        key = at("key", [P, GROUPS, E], F32, 4)
        onehot = at("onehot", [P, GROUPS, TOPK, E], F32, 4)
        onehotb = at("onehotb", [P, GROUPS, TOPK * E], BF16, 2)
        earlier = at("earlier", [P, GROUPS, TOPK * E], BF16, 2)
        chosen = at("chosen", [P, GROUPS, TOPK * E], F32, 4)
        rank_of_e = at("rank_of_e", [P, E], F32, 4)
        first_slot = at("first_slot", [P, E], F32, 4)
        red = at("red", [P, GROUPS], F32, 4)
        rsum = at("rsum", [P, GROUPS], F32, 4)
        weight = at("weight", [P, GROUPS, TOPK], F32, 4)
        place = at("place", [P, GROUPS, TOPK], F32, 4)
        place0 = at("place0", [P, GROUPS, TOPK], F32, 4)
        keep = at("keep", [P, GROUPS, TOPK], F32, 4)
        slot_of = at("slot_of", [P, GROUPS, TOPK], I32, 4)
        entry = at("entry", [P, GROUPS, TOPK, 2], I32, 4)
        empty = at("empty", [P, E * CH, 2], I32, 4)
        zrows = at("zrows", [P, 2 * D], BF16, 2)

        attention_over = [s_pv.now(), s_ST.now(), s_x2t.now(), s_logit.now(), s_xt.now(), s_out.now(),
                          s_x2r.now(), s_ph.now(), s_pl.now(), s_mrowc.now(), s_gate.now()]
        attention_over += [s.now() for s in s_x1st + s_x2st + s_stack]
        pool.wait(*attention_over)
        s_iota = signal("s_iota")
        s_fill = dma_signal("s_fill")
        pool.do(gp.iota, rank_of_e[:, :], pattern=[[-1, E]], base=E, channel_multiplier=0,
                allow_small_or_imprecise_dtypes=True, done=s_iota)
        pool.do(gp.iota, first_slot[:, :], pattern=[[SLOTS, E]], base=0, channel_multiplier=0,
                allow_small_or_imprecise_dtypes=True, done=s_iota)
        pool.do(gp.memset, empty[:, :, 1], 0, done=s_iota)
        pool.do(gp.iota, empty[:, :, 0], pattern=[[0, E * CH]], base=T, channel_multiplier=1, done=s_iota)
        for k in range(TOPK):
            pool.do(gp.iota, entry[:, :, k, 0], pattern=[[P, GROUPS]], base=0, channel_multiplier=1, done=s_iota)
        pool.do(gp.memset, zrows[:, :], 0.0, done=s_iota)
        iotas = s_iota.now()
        sp.wait(iotas)
        sp.do(nc.sync.dma_start, table.rearrange("(e p c) two -> p e (c two)", p=P, c=CH),
              empty[:, :, :].rearrange("p (e c) two -> p e (c two)", e=E), done=s_fill)
        sp.do(nc.sync.dma_start, xn_rows[T:T + P, :], zrows[:, :], done=s_fill)
        sp.do(nc.sync.dma_start, out[T:T + P, :], zrows[:, :].bitcast(F32), done=s_fill)
        filled = s_fill.now()

        def wide(ap):
            return ap.unsqueeze(2).to_broadcast([P, GROUPS, E])

        def over_groups(ap):
            return ap.unsqueeze(1).to_broadcast([P, GROUPS, E])

        dve.wait(iotas, s_logit.now(), *attention_over)
        lg = logits[:, :, :]
        step(dv.tensor_reduce, red[:, :], lg, X_AXIS, ALU.max)
        m = step(dv.tensor_tensor, probs[:, :, :], lg, wide(red[:, :]), ALU.subtract)
        act.wait(m)
        m = act.do(ac.activation, probs[:, :, :], probs[:, :, :], ACT.Exp, done=s_act)
        dve.wait(m)
        step(dv.tensor_reduce, rsum[:, :], probs[:, :, :], X_AXIS, ALU.add)
        step(dv.reciprocal, rsum[:, :], rsum[:, :])
        step(dv.tensor_tensor, probs[:, :, :], probs[:, :, :], wide(rsum[:, :]), ALU.mult)
        for k in range(TOPK):
            step(dv.tensor_reduce, weight[:, :, k], probs[:, :, :], X_AXIS, ALU.max)
            step(dv.tensor_tensor, key[:, :, :], probs[:, :, :], wide(weight[:, :, k]), ALU.is_ge)
            step(dv.tensor_tensor, key[:, :, :], key[:, :, :], over_groups(rank_of_e[:, :]), ALU.mult)
            step(dv.tensor_reduce, red[:, :], key[:, :, :], X_AXIS, ALU.max)
            step(dv.tensor_tensor, onehot[:, :, k, :], over_groups(rank_of_e[:, :]), wide(red[:, :]), ALU.is_equal)
            if k == 0:
                step(dv.scalar_tensor_tensor, probs[:, :, :], onehot[:, :, 0, :], -2.0, probs[:, :, :], ALU.mult, ALU.add)
        step(dv.tensor_copy, onehotb[:, :, :], onehot[:, :, :, :].rearrange("p g k e -> p g (k e)"))
        step(dv.memset, earlier[:, 0, :], 0.0)
        for g in range(1, GROUPS):
            step(dv.tensor_tensor, earlier[:, g, :], earlier[:, g - 1, :], onehotb[:, g - 1, :], ALU.add)
        s_place = signal("s_place")
        pe.wait(s_dve.now(), bank_free[7])
        n_all = GROUPS * TOPK * E
        pe.do(mm, bank(7)[:, 0:n_all], before[:, :], onehotb[:, :, :].rearrange("p g k -> p (g k)"), start=True, stop=False)
        m = pe.do(mm, bank(7)[:, 0:n_all], ones[:, :], earlier[:, :, :].rearrange("p g k -> p (g k)"), start=False, stop=True, done=s_place)
        dve.wait(m)
        oh = onehot[:, :, :, :].rearrange("p g k e -> p (g k e)")
        ch = chosen[:, :, :].rearrange("p g k -> p (g k)")
        gk = GROUPS * TOPK
        step(dv.tensor_tensor, ch, bank(7)[:, 0:n_all], oh, ALU.mult)
        bank_free[7] = s_dve.now()
        step(dv.tensor_reduce, place[:, :, :].rearrange("p g k -> p (g k)"), ch.rearrange("p (a e) -> p a e", e=E), X_AXIS, ALU.add)
        step(dv.tensor_tensor, ch.rearrange("p (a e) -> p a e", e=E), oh.rearrange("p (a e) -> p a e", e=E),
             first_slot[:, :].unsqueeze(1).to_broadcast([P, gk, E]), ALU.mult)
        step(dv.tensor_reduce, place0[:, :, :].rearrange("p g k -> p (g k)"), ch.rearrange("p (a e) -> p a e", e=E), X_AXIS, ALU.add)
        step(dv.tensor_scalar, keep[:, :, :], place[:, :, :], float(CAP), float(DROPPED), ALU.is_ge, ALU.mult)
        step(dv.tensor_tensor, place[:, :, :], place[:, :, :], place0[:, :, :], ALU.add)
        step(dv.tensor_tensor, place[:, :, :], place[:, :, :], keep[:, :, :], ALU.add)
        step(dv.tensor_copy, slot_of[:, :, 0], place[:, :, 0])
        step(dv.tensor_scalar, slot_of[:, :, 1], place[:, :, 1], float(CAP), None, ALU.add)
        m = step(dv.tensor_copy, entry[:, :, :, 1].bitcast(F32), weight[:, :, :])
        s_scatter = dma_signal("s_scatter")
        pool.wait(m, iotas, filled)
        for g in range(GROUPS):
            for k in range(TOPK):
                pool.do(gp.indirect_dma_start, out=table, out_offset=bass.IndirectOffsetOnAxis(ap=slot_of[:, g, k:k + 1], axis=0),
                        in_=entry[:, g, k, :], in_offset=None, bounds_check=E * SLOTS - 1, oob_is_err=False, done=s_scatter)
        s_table = dma_signal("s_table")
        sp.wait(s_scatter.now())
        m_slots = sp.do(nc.sync.dma_start, slots[:, :, :, :].rearrange("p e c two -> p e (c two)"),
                        table.rearrange("(e p c) two -> p e (c two)", p=P, c=CH), done=s_table)

        s_gather = dma_signal("s_gather")
        s_et, s_etc_h, s_etc_l = signal("s_et"), signal("s_etc_h"), signal("s_etc_l")
        HALVES = [(0, CAP), (CAP, CAP)]
        E_UNITS, E_YBANKS, E_TR = [0, 2], [4, 5], [6, 7]
        attention_over += [s_up.now(), m_slots, s_dve.now()]
        rows_stored = [s.now() for s in s_x2st]
        for queue in (pe, act, dve, pool, sp):
            queue.wait(*attention_over)
        expert_x, et_read = {}, {}

        def gather(e):
            pool.wait(m_slots, filled, *rows_stored)
            if e:
                pool.wait(et_mark[e - 1])
            for c in range(CH):
                pool.do(gp.indirect_dma_start, out=xg[:, c, :], out_offset=None, in_=xn_rows,
                        in_offset=bass.IndirectOffsetOnAxis(ap=slots[:, e, c, 0:1], axis=0), bounds_check=T + P - 1,
                        oob_is_err=True, done=s_gather)
            gathered[e] = s_gather.now()

        gathered, et_mark = {}, {}

        def transpose_slots(e):
            pe.wait(gathered[e])
            if e >= 2:
                act.wait(et_read[e - 2])
                dve.wait(et_read[e - 2])
            for c in range(CH):
                b = E_TR[c % 2]
                pe.wait(bank_free[b])
                view = bank(b).bitcast(BF16)
                for j in range(2 * KB):
                    pe.do(tr, view[:, j * P:j * P + P], xg[:, c, j * P:j * P + P], identb[:, :], done=s_et if j == 2 * KB - 1 else None)
                m = s_et.now()
                dst = slice(c * P, c * P + P)
                src = view.rearrange("p (a k t) -> p a k t", a=2, k=KB)
                act.wait(m)
                mh = act.do(ac.activation, eth[e % 2][:, :, dst], src[:, 0], ACT.Copy, done=s_etc_h)
                act.wait(mh)
                ml = act.do(ac.activation, etl[e % 2][:, :, dst], src[:, 1], ACT.Copy, done=s_etc_l)
                bank_free[b] = ml
            et_mark[e] = s_et.now()
            expert_x[e] = [s_etc_h.now(), s_etc_l.now()]

        def store_expert(e, c):
            def store(n, b):
                y = yout[n % 3]
                act.wait(m_slots)
                m = act.do(ac.activation, y[:, :], bank(b), ACT.Copy, scale=slots[:, e, c, 1:2].bitcast(F32), done=s_y)
                pool.wait(m, filled, *[s.now() for s in s_yst])
                return m, pool.do(gp.indirect_dma_start, out=out, out_offset=bass.IndirectOffsetOnAxis(ap=slots[:, e, c, 0:1], axis=0),
                                  in_=y[:, :], in_offset=None, bounds_check=T + P - 1, oob_is_err=True, compute_op=ALU.add,
                                  done=s_yst[n % 3])
            return store

        gather(0)
        stage_free.clear()
        stages = [s[:, :] for s in stage]
        order = [(e, f, w[e], q) for e in range(E) for f, w in ((w1_quarter, w1), (w2_quarter, w2)) for q in range(4)]
        LEAD = NST - 1
        pending = []

        def next_quarter(written_over):
            while len(pending) < len(order) and len(pending) <= quarter_at[0] + LEAD:
                _, f, w, q = order[len(pending)]
                pending.append(f(stages, w, q, []))
            quarter_at[0] += 1
            act.wait(written_over)
            dve.wait(written_over)
            return pending[quarter_at[0] - 1]()

        quarter_at = [0]
        w1_ready["next"] = [next_quarter(s_up.now()) for q in range(4)]
        rank_down_weights(wd[0], s_up.now())
        transpose_slots(0)
        for e in range(E):
            w1_ready["now"] = w1_ready["next"]
            pe.wait(*expert_x[e])
            hi, lo = eth[e % 2], etl[e % 2]
            w2_free = last_down[0]
            r = rank_features(hi, lo, HALVES, E_UNITS)
            rank_up_weights(wu[e], e, w2_free)
            if e + 1 < E:
                gather(e + 1)
            first = count["up"]
            w2_ready["now"] = []
            for fb in range(FB):
                if fb % 4 == 0:
                    w2_ready["now"].append(next_quarter(w2_free))
                up_block(hi, lo, HALVES, fb, E_UNITS, b1cols[:, e * FB + fb:e * FB + fb + 1], hh, hl)
            et_read[e] = s_up.now()
            w1_free = s_up.now()
            w1_ready["next"] = []
            for c in range(CH):
                if c < 4 and e + 1 < E:
                    w1_ready["next"].append(next_quarter(w1_free))
                for _ in down_chunk(c, first, r, E_YBANKS, store_expert(e, c), hh, hl):
                    pass
                if c == 1 and e + 1 < E:
                    rank_down_weights(wd[e + 1], w1_free)
                if c == 2 and e + 1 < E:
                    transpose_slots(e + 1)
            low_read[r] = last_down[0]
        sp.wait(*[s.now() for s in s_yst + s_x1st + s_x2st + [s_fill, s_scatter]])

        block = stack.enter_context(nc.Block())

        @block.sync
        def _(engine):
            sp.issue(engine)

        @block.gpsimd
        def _(engine):
            pool.issue(engine)

        @block.scalar
        def _(engine):
            act.issue(engine)

        @block.vector
        def _(engine):
            dve.issue(engine)

        @block.tensor
        def _(engine):
            pe.issue(engine)


_INPUTS = ["x", "ctx_2048", "itok_B_779_1933", "L0_ffn_gate_w", "L0_ffn_w1", "L0_ffn_b1", "L0_ffn_w2", "L0_ffn_b2",
           "L0_ffn_wd", "L0_ffn_wu", "L0_ffn_sw1", "L0_ffn_sb1", "L0_ffn_sw2", "L0_ffn_sb2", "L0_ffn_swd", "L0_ffn_swu"]


def kernel(**inputs):
    import concourse.bacc as bacc
    from concourse.bass_utils import run_bass_kernel_spmd

    nc = bacc.Bacc("TRN2", target_bir_lowering=False, num_devices=1, dynamic_dma_scratch_size=8192)
    arrays, args = {}, []
    for name in _INPUTS:
        a = np.ascontiguousarray(inputs[name])
        arrays[f"in_{name}"] = a
        args.append(nc.dram_tensor(f"in_{name}", a.shape, mybir.dt.from_np(a.dtype), kind="ExternalInput").ap())
    out = nc.dram_tensor("out_rows", (T + P, D), F32, kind="ExternalOutput").ap()
    build(nc, *args, out)
    r = run_bass_kernel_spmd(nc, [arrays], core_ids=[0])
    return r.results[0]["out_rows"][:T].reshape(B, C, L)
```

```python
from contextlib import ExitStack

import concourse.bass as bass
from concourse import mybir

import numpy as np

F32 = mybir.dt.float32
BF16 = mybir.dt.bfloat16
I32 = mybir.dt.int32
ALU = mybir.AluOpType
ACT = mybir.ActivationFunctionType
X_AXIS = mybir.AxisListType.X

P = 128
B, C, L = 8, 256, 512
T, D = B * C, L
HEADS, HD = 8, 32
GROUPS = T // P
GH = P // HD
QT = L // P
SCALE = 1.0 / (64 ** 0.5 * float(np.log(20)))
EPS = 1e-5
E, TOPK, RANK = 8, 2, 32
F = 4 * D
CAP = int(T * 1.25 / E)
SLOTS = TOPK * CAP
CH = SLOTS // P
KB, FB = D // P, F // P
PASS = 256
GPP = PASS // P
DROPPED = 1 << 14
WIDE = RANK * 3


class Signal:

    def __init__(self, sem, step):
        self.sem, self.step, self.value = sem, step, 0

    def now(self):
        return self, self.value


class Queue:

    def __init__(self):
        self.items, self.passed = [], {}

    def wait(self, *marks):
        for signal, value in marks:
            if self.passed.get(signal, 0) < value:
                self.passed[signal] = value
                self.items.append((None, signal.sem, value, None))

    def do(self, instruction, *args, done=None, **kwargs):
        self.items.append((instruction, args, kwargs, done))
        if done is not None:
            done.value += done.step
            return done.now()

    def issue(self, engine):
        for instruction, a, b, done in self.items:
            if instruction is None:
                engine.wait_ge(a, b)
            else:
                issued = instruction(*a, **b)
                if done is not None:
                    issued.then_inc(done.sem, done.step)


def build(nc, x, ctx_in, itok, gate_w, w1, b1, w2, b2, wd, wu, sw1, sb1, sw2, sb2, swd, swu, out):
    stack = ExitStack()
    with stack:
        def sb(name, shape, dt):
            return stack.enter_context(nc.sbuf_tensor(name, shape, dt))

        def signal(name, step=1):
            return Signal(stack.enter_context(nc.semaphore(name)), step)

        def dma_signal(name):
            return signal(name, 16)

        pe, act, dve, pool, sp = Queue(), Queue(), Queue(), Queue(), Queue()
        mm, tr = nc.tensor.matmul, nc.tensor.transpose
        dv, ac, gp = nc.vector, nc.scalar, nc.gpsimd

        x_rows = x.rearrange("b c l -> (b c) l")
        ctx_rows = ctx_in.rearrange("b c l -> (b c) l")
        parts_dram = nc.dram_tensor("split_parts", [2, 4, P, L], BF16, kind="Internal").ap()
        xn_rows = nc.dram_tensor("normed_rows", [T + P, 2 * D], BF16, kind="Internal").ap()
        table = nc.dram_tensor("slot_table", [E * SLOTS, 2], I32, kind="Internal").ap()

        w1h, w1l = sb("w1h", [P, KB, F], BF16), sb("w1l", [P, KB, F], BF16)
        w2h, w2l = sb("w2h", [P, FB, D], BF16), sb("w2l", [P, FB, D], BF16)
        wdf = sb("wdf", [P, KB, RANK], F32)
        wdh, wdl = sb("wdh", [P, KB, WIDE], BF16), sb("wdl", [P, KB, WIDE], BF16)
        wuf, wus = sb("wuf", [WIDE, D], F32), sb("wus", [P, D], BF16)
        hidden = sb("hidden", [P, 2 * FB * SLOTS], BF16)
        hh, hl = (hidden[:, k * FB * SLOTS:(k + 1) * FB * SLOTS].rearrange("p (f n) -> p f n", n=SLOTS) for k in range(2))
        hf = [sb(f"hf{i}", [P, SLOTS], F32) for i in range(2)]
        low = [sb(f"low{i}", [P, SLOTS], BF16) for i in range(2)]
        lowf = sb("lowf", [WIDE, SLOTS], F32)
        yout = [sb(f"yout{i}", [P, D], F32) for i in range(3)]
        ident = sb("ident", [P, P], F32)
        identb = sb("identb", [P, P], BF16)
        before = sb("before", [P, P], BF16)
        ones = sb("ones", [P, P], BF16)
        half = sb("half", [P, 1], F32)
        b1rows, b1cols = sb("b1rows", [P, P], F32), sb("b1cols", [P, E * FB], F32)
        sb1rows, sb1cols = sb("sb1rows", [FB, P], F32), sb("sb1cols", [P, FB], F32)
        b2f = sb("b2f", [E + 1, D], F32)
        b2parts = sb("b2parts", [E + 1, 3, D], BF16)
        gate = sb("gate", [P, KB, E], F32)
        logits = sb("logits", [P, GROUPS, E], F32)
        slots = sb("slots", [P, E, CH, 2], I32)

        base = nc.sbuf_base
        offset = [base + (-base) % 64]
        limit = nc.sbuf_usable_end

        def at(name, shape, dt, size):
            n = size
            for s in shape[1:]:
                n *= s
            t = nc.alloc_sbuf_tensor_at(name, shape, dt, offset=offset[0])
            offset[0] += n + (-n) % 64
            if offset[0] > limit:
                raise ValueError(f"{name} ends at {offset[0]}, {limit} is the limit")
            return t

        xth = [at(f"xth{i}", [P, KB, PASS], BF16, 2) for i in range(2)]
        xtl = [at(f"xtl{i}", [P, KB, PASS], BF16, 2) for i in range(2)]
        gathered_start = offset[0]
        NX, NS = 4, 4
        xin = [at(f"xin{i}", [P, L], F32, 4) for i in range(NX)]
        cin = [at(f"cin{i}", [P, L], F32, 4) for i in range(2)]
        xn = at("xn", [P, L], F32, 4)
        routing_start = offset[0]
        QS = [at(f"QS{i}", [P, GH, L], BF16, 2) for i in range(NS)]
        KS = [at(f"KS{i}", [P, GH, L], BF16, 2) for i in range(NS)]
        VT = [at(f"VT{i}", [P, 2, QT, P], BF16, 2) for i in range(2)]
        prob = [at(f"prob{i}", [P, L], F32, 4) for i in range(3)]
        shh, shl = (hidden[:, k * FB * PASS:(k + 1) * FB * PASS].rearrange("p (f n) -> p f n", n=PASS) for k in range(2))
        NPH = 8
        spare = hidden[:, 2 * FB * PASS:2 * FB * PASS + 2 * NPH * L].rearrange("p (n l) -> p n l", l=L)
        ph = [spare[:, i, :] for i in range(NPH)]
        pl = [spare[:, NPH + i, :] for i in range(NPH)]
        split = [hidden[:, 2 * FB * PASS + (2 * NPH + 4 * i) * L:][:, 0:4 * L].rearrange("p (n l) -> p n l", l=L) for i in range(2)]
        rowmax = [at(f"rowmax{i}", [P, GH * QT], F32, 4) for i in range(2)]
        MS = at("MS", [P, GH * QT, HD], BF16, 2)
        rden = at("rden", [P, L], F32, 4)
        x2s = [at(f"x2_{i}", [P, L], F32, 4) for i in range(2)]
        x2r = [at(f"x2r{i}", [P, 2, L], BF16, 2) for i in range(2)]
        x2t = at("x2t", [P, KB, P], F32, 4)
        stat = at("stat", [P, 2, 6], F32, 4)
        mv = at("mv", [P, 2, 4], F32, 4)
        scale_i = at("scale_i", [P, B], I32, 4)
        scale_f = at("scale_f", [P, B], F32, 4)
        scales = at("scales", [P, B], F32, 4)

        offset[0] = routing_start
        NST = 3
        stage = [at(f"stage{i}", [P, 2048], F32, 4) for i in range(NST)]
        eth = [at(f"eth{i}", [P, KB, SLOTS], BF16, 2) for i in range(2)]
        etl = [at(f"etl{i}", [P, KB, SLOTS], BF16, 2) for i in range(2)]
        offset[0] = gathered_start
        xg = at("xg", [P, CH, 2 * D], BF16, 2)
        PB = stack.enter_context(nc.psum_tensor("banks", [P, 8, 512], F32))

        def bank(i):
            return PB[:, i, :]

        s_const = signal("s_const")
        s_pool = signal("s_pool")
        s_dve = signal("s_dve")
        s_act = signal("s_act")

        def fill(view, value):
            pool.do(gp.memset, view, value, done=s_pool)
            pool.wait(s_pool.now())

        fill(ident[:, :], 0.0)
        pool.do(gp.affine_select, out=ident[:, :], in_=ident[:, :], compare_op=ALU.not_equal, fill=1.0,
                base=0, pattern=[[-1, P]], channel_multiplier=1, done=s_pool)
        pool.wait(s_pool.now())
        pool.do(gp.tensor_copy, identb[:, :], ident[:, :], done=s_const)
        fill(before[:, :], 0.0)
        pool.do(gp.affine_select, out=before[:, :], in_=before[:, :], compare_op=ALU.is_ge, fill=1.0,
                base=0, pattern=[[-1, P]], channel_multiplier=1, done=s_const)
        pool.wait(s_const.now())
        fill(ones[:, :], 1.0)
        fill(half[:, :], -0.5)
        fill(MS[:, :, :], 0.0)
        constants = s_pool.now()
        for queue in (dve, pe, act):
            queue.wait(s_const.now(), constants)

        def step(*args, **kwargs):
            mark = dve.do(*args, done=s_dve, **kwargs)
            dve.wait(mark)
            return mark

        def chain():
            last = []

            def link(*args, done=s_dve, **kwargs):
                dve.wait(*last)
                last[:] = [dve.do(*args, done=done, **kwargs)]
                return last[0]
            return link

        s_x = [dma_signal(f"s_x{i}") for i in range(NX)]
        s_c = [dma_signal(f"s_c{i}") for i in range(2)]
        s_rstd = signal("s_rstd")
        s_split = signal("s_split")
        s_khi = signal("s_khi")
        s_parts = dma_signal("s_parts")
        s_stack = [dma_signal(f"s_stack{i}") for i in range(NS)]
        s_vt, s_vtc = signal("s_vt"), signal("s_vtc")
        s_phv = signal("s_phv")
        s_plv = signal("s_plv")
        s_S, s_max = signal("s_S"), signal("s_max")
        s_ms, s_mrow, s_mrowc = signal("s_ms"), signal("s_mrow"), signal("s_mrowc")
        s_ST, s_exp, s_ph, s_pl, s_pv = (signal(n) for n in ("s_ST", "s_exp", "s_ph", "s_pl", "s_pv"))
        s_out = signal("s_out")
        s_x1st = [dma_signal(f"s_x1st{i}") for i in range(GROUPS)]
        s_x2r = signal("s_x2r")
        s_x2st = [dma_signal(f"s_x2st{i}") for i in range(2)]
        s_x2t, s_x2tc = signal("s_x2t"), signal("s_x2tc")
        s_gate, s_logit, s_xt = signal("s_gate"), signal("s_logit"), signal("s_xt")

        x_loaded, c_loaded, split_done, khi_done, stacked, vt_done = {}, {}, {}, {}, {}, {}
        st_done, mrow_done, out_done, x1_stored, x2_stored = {}, {}, {}, {}, {}
        xt_ready = {}
        bank_free = {i: constants for i in range(8)}

        def layer_norm(src, dst, k, link):
            link(dv.bn_stats, stat[:, k, :], src)
            yield
            link(dv.bn_aggr, mv[:, k, 0:2], stat[:, k, :])
            yield
            m = link(dv.tensor_scalar, mv[:, k, 2:3], mv[:, k, 1:2], EPS, None, ALU.add)
            pool.wait(m)
            m = pool.do(gp.tensor_tensor, mv[:, k, 3:4], mv[:, k, 2:3], half[:, :], ALU.pow, done=s_rstd)
            for _ in range(4):
                yield
            dve.wait(m)
            link(dv.tensor_scalar, dst, src, mv[:, k, 0:1], mv[:, k, 3:4], ALU.subtract, ALU.mult)
            yield

        def load_group(g):
            rows = slice(P * g, P * g + P)
            if g >= NX:
                sp.wait(x2_done[g - NX], x1_stored[g - NX])
            x_loaded[g] = sp.do(nc.sync.dma_start, xin[g % NX][:, :], x_rows[rows, :], done=s_x[g % NX])
            if g >= 2:
                sp.wait(split_done[g - 2], khi_done[g - 2])
            c_loaded[g] = sp.do(nc.sync.dma_start, cin[g % 2][:, :], ctx_rows[rows, :], done=s_c[g % 2])

        def prepare(g):
            s, part = g % NS, split[g % 2]
            if g >= 2:
                dve.wait(stacked[g - 2])
                act.wait(stacked[g - 2])
                act.wait(vt_done[g - 2])
                dve.wait(vt_done[g - 2])
            link = chain()
            dve.wait(x_loaded[g])
            if g:
                dve.wait(split_done[g - 1])
            yield from layer_norm(xin[g % NX][:, :], xn[:, :], 0, link)
            link(dv.tensor_copy, part[:, 0, :], xn[:, :])
            act.wait(c_loaded[g])
            khi_done[g] = act.do(ac.activation, part[:, 2, :], cin[g % 2][:, :], ACT.Copy, done=s_khi)
            yield
            link(dv.tensor_tensor, part[:, 1, :], xn[:, :], part[:, 0, :], ALU.subtract, done=s_split)
            yield
            dve.wait(khi_done[g], c_loaded[g])
            split_done[g] = dve.do(dv.tensor_tensor, part[:, 3, :], cin[g % 2][:, :], part[:, 2, :],
                                   ALU.subtract, done=s_split)
            yield
            if g >= NS:
                sp.wait(st_done[g - NS])
            sp.wait(split_done[g], khi_done[g])
            if g >= 2:
                sp.wait(stacked[g - 2])
            sp.wait(sp.do(nc.sync.dma_start, parts_dram[g % 2].rearrange("a p c -> p a c"), part[:, :, :], done=s_parts))
            for dst, parts in ((QS[s], (0, 1, 0)), (KS[s], (2, 2, 3))):
                for k, which in enumerate(parts):
                    sp.do(nc.sync.dma_start, dst[HD * k:HD * k + HD, :, :],
                          parts_dram[g % 2, which].rearrange("(h p) c -> p h c", p=HD), done=s_stack[s])
            stacked[g] = s_stack[s].now()
            yield

        def transpose_values(g, b):
            pe.wait(split_done[g], khi_done[g], bank_free[b])
            view = bank(b).bitcast(BF16)
            for k in range(2):
                for t in range(QT):
                    at_ = (k * QT + t) * P
                    pe.do(tr, view[:, at_:at_ + P], split[g % 2][:, 2 + k, t * P:t * P + P], identb[:, :],
                          done=s_vt if (k, t) == (1, QT - 1) else None)
            vt_done[g] = s_vt.now()
            act.wait(vt_done[g])
            if g >= 2:
                act.wait(pv_done[g - 2])
            bank_free[b] = act.do(ac.activation, VT[g % 2][:, :, :, :].rearrange("p a t c -> p (a t c)"), view[:, :],
                                  ACT.Copy, done=s_vtc)
            vtc_done[g] = bank_free[b]

        pv_done, vtc_done = {}, {}

        def score_max(g, i, b):
            h, t = divmod(i, QT)
            s = g % NS
            pe.wait(stacked[g], bank_free[b])
            m = pe.do(mm, bank(b), QS[s][0:96, h, t * P:t * P + P], KS[s][0:96, h, :], start=True, stop=True, done=s_S)
            dve.wait(m)
            bank_free[b] = dve.do(dv.reduce_max, rowmax[g % 2][:, i:i + 1], bank(b), X_AXIS, done=s_max)

        ms_done = {}

        def max_parts(g):
            dve.wait(s_max.now())
            if g:
                dve.wait(mrow_done[g - 1])
            mx = rowmax[g % 2][:, :]
            step(dv.tensor_scalar, MS[:, :, 0], mx, -1.0, None, ALU.mult)
            ms_done[g] = dve.do(dv.scalar_tensor_tensor, MS[:, :, 1], mx, -1.0, MS[:, :, 0], ALU.mult, ALU.subtract, done=s_ms)

        def max_rows(g, b):
            s = g % NS
            pe.wait(ms_done[g], bank_free[b], filled_late[0])
            for t in range(QT):
                for h in range(GH):
                    last = (t, h) == (QT - 1, GH - 1)
                    pe.do(mm, bank(b)[HD * h:HD * h + HD, t * P:t * P + P], MS[:, h * QT + t, :], identb[:, :],
                          start=True, stop=True, done=s_mrow if last else None)
            mrow_done[g] = s_mrow.now()
            for h in range(GH):
                yield
                act.wait(mrow_done[g])
                act.do(ac.activation, QS[s][96:P, h, :], bank(b)[HD * h:HD * h + HD, :], ACT.Copy, done=s_mrowc)
            bank_free[b] = s_mrowc.now()
            mrowc_done[g] = bank_free[b]

        mrowc_done, filled_late = {}, []
        tick = {"st": 0}
        ph_mark, pl_mark, ph_read = {}, {}, {}

        def exponentials(g, i, b):
            t, h = divmod(i, GH)
            s, n = g % NS, tick["st"]
            tick["st"] += 1
            pe.wait(stacked[g], mrowc_done[g], bank_free[b])
            m = pe.do(mm, bank(b), KS[s][:, h, t * P:t * P + P], QS[s][:, h, :], start=True, stop=True, done=s_ST)
            act.wait(m)
            if n >= 3:
                act.wait(ph_mark[n - 3], pl_mark[n - 3])
            m = act.do(ac.activation, prob[n % 3][:, :], bank(b), ACT.Exp, scale=scales[:, g // 2:g // 2 + 1], done=s_exp)
            bank_free[b] = m
            if n >= NPH:
                (dve if n % 2 else act).wait(ph_read[n - NPH])
                pool.wait(ph_read[n - NPH])
            if n % 2:
                dve.wait(m)
                ph_mark[n] = dve.do(dv.tensor_copy, ph[n % NPH], prob[n % 3][:, :], done=s_phv)
            else:
                act.wait(m)
                ph_mark[n] = act.do(ac.activation, ph[n % NPH], prob[n % 3][:, :], ACT.Copy, done=s_ph)
            if n % 4 == 3:
                dve.wait(ph_mark[n])
                pl_mark[n] = dve.do(dv.tensor_tensor, pl[n % NPH], prob[n % 3][:, :], ph[n % NPH], ALU.subtract, done=s_plv)
            else:
                pool.wait(ph_mark[n], m)
                pl_mark[n] = pool.do(gp.tensor_tensor, pl[n % NPH], prob[n % 3][:, :], ph[n % NPH],
                                     ALU.subtract, done=s_pl)
            if i == GH * QT - 1:
                st_done[g] = s_ST.now()

        def weighted_values(g, t, b_out, b_sum):
            n0 = g * GH * QT + t * GH
            v = VT[g % 2]
            pe.wait(vtc_done[g], ph_mark[n0 + GH - 2], ph_mark[n0 + GH - 1])
            if t == 0:
                pe.wait(bank_free[b_out], bank_free[b_sum])
            work = [(b_sum, None, ph), (b_out, 0, ph), (b_out, 1, ph), (b_sum, None, pl), (b_out, 0, pl)]
            opened = set()
            for k, (b, part, src) in enumerate(work):
                if src is pl:
                    pe.wait(pl_mark[n0 + GH - 2], pl_mark[n0 + GH - 1])
                for h in range(GH):
                    cols = slice(HD * h, HD * h + HD)
                    lhsT = ones[:, 0:HD] if part is None else v[:, part, t, cols]
                    last = (k, h) == (len(work) - 1, GH - 1)
                    pe.do(mm, bank(b)[cols, :], lhsT, src[(n0 + h) % NPH],
                          start=t == 0 and b not in opened, stop=t == QT - 1 and k >= 3, done=s_pv if last else None)
                opened.add(b)
                if k == len(work) - 1:
                    for h in range(GH):
                        ph_read[n0 + h] = s_pv.now()
                    if t == QT - 1:
                        pv_done[g] = s_pv.now()
                yield

        def finish_attention(g, b_out, b_sum):
            rows = slice(P * g, P * g + P)
            link = chain()
            dve.wait(pv_done[g])
            if g:
                dve.wait(out_done[g - 1])
            for q in range(QT):
                cols = slice(q * P, q * P + P)
                link(dv.reciprocal, rden[:, cols], bank(b_sum)[:, cols])
                yield
            bank_free[b_sum] = s_dve.now()
            o = xin[g % NX]
            bank_free[b_out] = link(dv.tensor_tensor, rden[:, :], bank(b_out), rden[:, :], ALU.mult)
            yield
            out_done[g] = link(dv.tensor_tensor, o[:, :], o[:, :], rden[:, :], ALU.add, done=s_out)
            sp.wait(out_done[g])
            x1_stored[g] = sp.do(nc.sync.dma_start, out[rows, :], o[:, :], done=s_x1st[g])
            yield
            x2 = x2s[g % 2]
            if g >= 2:
                dve.wait(x2t_done[g - 2])
            yield from layer_norm(o[:, :], x2[:, :], 1, link)
            x2_done[g] = s_dve.now()
            if g >= 2:
                dve.wait(x2_stored[g - 2])
            r = x2r[g % 2]
            link(dv.tensor_copy, r[:, 0, :], x2[:, :])
            yield
            m = link(dv.tensor_tensor, r[:, 1, :], x2[:, :], r[:, 0, :], ALU.subtract, done=s_x2r)
            sp.wait(m)
            x2_stored[g] = sp.do(nc.sync.dma_start, xn_rows[rows, :], r[:, :, :].rearrange("p a d -> p (a d)"), done=s_x2st[g % 2])
            yield

        x2t_done, x2_done = {}, {}

        def transpose_tokens(g, b):
            p, col = g // GPP, (g % GPP) * P
            x2 = x2s[g % 2]
            pe.wait(x2_done[g], bank_free[b])
            for k in range(KB):
                pe.do(tr, bank(b)[:, k * P:k * P + P], x2[:, k * P:k * P + P], ident[:, :], done=s_x2t if k == KB - 1 else None)
            x2t_done[g] = s_x2t.now()
            act.wait(x2t_done[g])
            if g:
                act.wait(xt_ready[g - 1], gate_done[g - 1])
            m = act.do(ac.activation, x2t[:, :, :].rearrange("p k t -> p (k t)"), bank(b), ACT.Copy, done=s_x2tc)
            for _ in range(3):
                yield
            pe.wait(m)
            for k in range(KB):
                pe.do(mm, bank(b)[:, 0:E], x2t[:, k, :], gate[:, k, :], start=k == 0, stop=k == KB - 1,
                      done=s_gate if k == KB - 1 else None)
            gate_done[g] = s_gate.now()
            hi, lo = xth[p % 2][:, :, col:col + P], xtl[p % 2][:, :, col:col + P]
            dve.wait(m)
            if p >= 2:
                dve.wait(pass_up_done[p - 2])
            link = chain()
            link(dv.tensor_copy, hi, x2t[:, :, :])
            yield
            xt_ready[g] = link(dv.tensor_tensor, lo, x2t[:, :, :], hi, ALU.subtract, done=s_xt)
            yield
            dve.wait(gate_done[g])
            bank_free[b] = dve.do(dv.tensor_copy, logits[:, g, :], bank(b)[:, 0:E], done=s_logit)

        gate_done, pass_up_done = {}, {}

        s_up, s_gelu, s_hh, s_hl = signal("s_up"), signal("s_gelu"), signal("s_hh"), signal("s_hl")
        s_hha, s_hlp = signal("s_hha"), signal("s_hlp")
        s_down, s_y = signal("s_down"), signal("s_y")
        s_yst = [dma_signal(f"s_yst{i}") for i in range(3)]
        b2_parts_ready = []
        count = {"up": 0, "down": 0, "rank": 0}
        gelu_mark, h_split, low_done, y_stored = {}, {}, {}, {}
        low_read = {}
        last_down = [constants]
        w1_ready, w2_ready, wd_ready, wu_ready = {}, {}, {}, {}

        def rank_features(x_hi, x_lo, halves, units):
            n = count["rank"]
            count["rank"] += 1
            b0 = units[count["up"] % len(units)]
            count["up"] += 1
            pe.wait(wd_ready["now"], *[bank_free[b0 + j] for j in range(len(halves))])
            for j, (c0, w) in enumerate(halves):
                k = 0
                for weights, data in ((wdh, x_hi), (wdh, x_lo), (wdl, x_hi)):
                    for kb in range(KB):
                        k += 1
                        pe.do(mm, bank(b0 + j)[0:WIDE, 0:w], weights[:, kb, :], data[:, kb, c0:c0 + w],
                              start=k == 1, stop=k == 3 * KB, done=s_up if (j, k) == (len(halves) - 1, 3 * KB) else None)
            act.wait(s_up.now())
            w, total = halves[0][1], sum(w for _, w in halves)
            if n:
                act.wait(low_done[n - 1])
            m = act.do(ac.activation, lowf[:, 0:total].rearrange("p (j w) -> p j w", w=w), PB[0:WIDE, b0:b0 + len(halves), 0:w],
                       ACT.Gelu, done=s_gelu)
            for j in range(len(halves)):
                bank_free[b0 + j] = m
            o = low[n % 2]
            dve.wait(m)
            if n >= 2:
                dve.wait(low_read[n - 2])
            step(dv.tensor_copy, o[0:WIDE, 0:total], lowf[:, 0:total])
            low_done[n] = step(dv.tensor_tensor, o[HD:2 * HD, 0:total], lowf[HD:2 * HD, 0:total], o[HD:2 * HD, 0:total], ALU.subtract)
            return n

        def up_block(x_hi, x_lo, halves, fb, units, bias, hh, hl, shared=False):
            n = count["up"]
            count["up"] += 1
            b0 = units[n % len(units)]
            pe.wait(w1_ready["now"][fb // 4], *[bank_free[b0 + j] for j in range(len(halves))])
            f0 = fb * P
            k = 0
            for weights, data in ((w1h, x_hi), (w1h, x_lo), (w1l, x_hi)):
                for kb in range(KB):
                    k += 1
                    for j, (c0, w) in enumerate(halves):
                        pe.do(mm, bank(b0 + j)[:, 0:w], weights[:, kb, f0:f0 + P], data[:, kb, c0:c0 + w],
                              start=k == 1, stop=k == 3 * KB, done=s_up if (j, k) == (len(halves) - 1, 3 * KB) else None)
            act.wait(s_up.now())
            w, total = halves[0][1], sum(w for _, w in halves)
            ring = 4 if total <= SLOTS // 2 else 2
            if n - ring in h_split:
                act.wait(h_split[n - ring])
            h_out = hf[n % 2][:, (n % ring) // 2 * total:][:, 0:total]
            m = act.do(ac.activation, h_out.rearrange("p (j w) -> p j w", w=w),
                       PB[:, b0:b0 + len(halves), 0:w], ACT.Gelu, bias=bias, done=s_gelu)
            for j in range(len(halves)):
                bank_free[b0 + j] = m
            if shared:
                act.wait(m, last_down[0])
                m = act.do(ac.activation, hh[:, fb, 0:total], h_out, ACT.Copy, done=s_hha)
                pool.wait(m, last_down[0])
                h_split[n] = pool.do(gp.tensor_tensor, hl[:, fb, 0:total], h_out, hh[:, fb, 0:total],
                                     ALU.subtract, done=s_hlp)
            else:
                dve.wait(m, last_down[0])
                dve.wait(dve.do(dv.tensor_copy, hh[:, fb, 0:total], h_out, done=s_hh))
                h_split[n] = dve.do(dv.tensor_tensor, hl[:, fb, 0:total], h_out, hh[:, fb, 0:total],
                                    ALU.subtract, done=s_hl)
            return n

        def down_chunk(c, first_up, rank_n, ybanks, store, hh, hl):
            n = count["down"]
            count["down"] += 1
            b = ybanks[n % len(ybanks)]
            cols = slice(c * P, c * P + P)
            pe.wait(bank_free[b], low_done[rank_n], *wu_ready["now"])
            pe.do(mm, bank(b), low[rank_n % 2][:, cols], wus[:, :], start=True, stop=False)
            for fb in range(FB):
                pe.wait(h_split[first_up + fb], w2_ready["now"][fb // 4])
                for k, (a, w) in enumerate(((hh, w2h), (hh, w2l), (hl, w2h))):
                    last = (fb, k) == (FB - 1, 2)
                    pe.do(mm, bank(b), a[:, fb, cols], w[:, fb, :], start=False, stop=last, done=s_down if last else None)
                yield
            last_down[0] = down = s_down.now()
            yield
            act.wait(down)
            if n >= 3:
                act.wait(y_stored[n - 3])
            bank_free[b], y_stored[n] = store(n, b)

        s_stage = [dma_signal(f"s_stage{i}") for i in range(NST)]
        s_wd, s_wu = dma_signal("s_wd"), dma_signal("s_wu")
        s_rankb = dma_signal("s_rankb")
        s_whi, s_wlo, s_wlog = signal("s_whi"), signal("s_wlo"), signal("s_wlog")
        count["stage"] = 0
        stage_free = {}

        def load_weights(stages, src, dst_hi, dst_lo, written_over):
            n = count["stage"]
            count["stage"] += 1
            i = n % len(stages)
            sp.wait(*stage_free.get(i, []))
            a, w = src.shape[1], src.shape[2]
            buf = stages[i].rearrange("p (a w) -> p a w", w=w)
            m = sp.do(nc.sync.dma_start, buf, src, done=s_stage[i])

            def split_them(by_gpsimd=False):
                act.wait(m, *written_over)
                hi = act.do(ac.activation, dst_hi, buf, ACT.Copy, done=s_whi)
                if by_gpsimd:
                    pool.wait(m, hi, *written_over)
                    lo = pool.do(gp.tensor_tensor, dst_lo, buf, dst_hi, ALU.subtract, done=s_wlog)
                else:
                    dve.wait(m, hi, *written_over)
                    lo = dve.do(dv.tensor_tensor, dst_lo, buf, dst_hi, ALU.subtract, done=s_wlo)
                stage_free[i] = [hi, lo]
                return lo
            return split_them

        def w1_quarter(stages, w, q, written_over):
            cols = slice(q * 512, q * 512 + 512)
            return load_weights(stages, w.rearrange("(k p) f -> p k f", p=P)[:, :, cols], w1h[:, :, cols], w1l[:, :, cols], written_over)

        def w2_quarter(stages, w, q, written_over):
            rows = slice(q * 4, q * 4 + 4)
            return load_weights(stages, w.rearrange("(k p) d -> p k d", p=P)[:, rows, :], w2h[:, rows, :], w2l[:, rows, :], written_over)

        def rank_down_weights(w, written_over):
            sp.wait(written_over, *stage_free.get("wd", []))
            m = sp.do(nc.sync.dma_start, wdf[:, :, :], w.rearrange("(k p) r -> p k r", p=P), done=s_wd)
            dve.wait(m, written_over)
            for j in range(3):
                step(dv.tensor_copy, wdh[:, :, j * RANK:(j + 1) * RANK], wdf[:, :, :])
            for j in range(3):
                step(dv.tensor_tensor, wdl[:, :, j * RANK:(j + 1) * RANK], wdf[:, :, :], wdh[:, :, j * RANK:(j + 1) * RANK], ALU.subtract)
            stage_free["wd"] = [s_dve.now()]
            wd_ready["now"] = s_dve.now()

        def rank_up_weights(w, bias_row, written_over):
            sp.wait(written_over, *b2_parts_ready, *stage_free.get("wu", []))
            for j in range(3):
                sp.do(nc.sync.dma_start, wuf[j * RANK:(j + 1) * RANK, :], w, done=s_wu)
            wu_loaded = s_wu.now()
            for j in range(3):
                sp.do(nc.sync.dma_start, wus[96 + j:97 + j, :], b2parts[bias_row:bias_row + 1, j, :], done=s_rankb)
            dve.wait(wu_loaded, written_over)
            step(dv.tensor_copy, wus[0:WIDE, :], wuf[:, :])
            m = step(dv.tensor_tensor, wus[64:96, :], wuf[64:96, :], wus[64:96, :], ALU.subtract)
            stage_free["wu"] = [m]
            wu_ready["now"] = [m, s_rankb.now()]

        hstage = [hidden[:, k * FB * PASS:(k + 1) * FB * PASS].bitcast(F32) for k in range(2)]

        def shared_weights():
            w1_ready["now"], w2_ready["now"] = [], []
            quarters = [(w1_quarter, sw1, q, w1_ready) for q in range(4)] + [(w2_quarter, sw2, q, w2_ready) for q in range(4)]
            loads = [f(hstage, w, q, [constants]) for f, w, q, _ in quarters[:2]]
            yield
            for k, quarter in enumerate(quarters):
                quarter[3]["now"].append(loads[k](by_gpsimd=True))
                if k + 2 < len(quarters):
                    f, w, q, _ = quarters[k + 2]
                    loads.append(f(hstage, w, q, [constants]))
                yield
            rank_down_weights(swd, constants)
            rank_up_weights(swu, E, constants)
            yield


        def store_shared(p, c):
            def store(n, b):
                y = yout[n % 3]
                m = act.do(ac.activation, y[:, :], bank(b), ACT.Copy, scale=0.2, done=s_y)
                rows = slice((p * GPP + c) * P, (p * GPP + c) * P + P)
                pool.wait(m, x1_stored[p * GPP + c])
                return m, pool.do(gp.dma_start, out[rows, :], y[:, :], accum_op=ALU.add, done=s_yst[n % 3])
            return store

        FFN_BANKS = [6, 7]
        pass_state = {}

        def shared_up(p, helped=True):
            hi, lo = xth[p % 2], xtl[p % 2]
            pe.wait(*[xt_ready[p * GPP + i] for i in range(GPP)])
            halves = [(0, PASS)]
            r = rank_features(hi, lo, halves, FFN_BANKS)
            pass_state[p] = (count["up"], r)
            yield
            for fb in range(FB):
                up_block(hi, lo, halves, fb, FFN_BANKS, sb1cols[:, fb:fb + 1], shh, shl, shared=helped)
                yield
            pass_up_done[p] = s_up.now()

        def shared_down(p):
            first, r = pass_state[p]
            for c in range(GPP):
                yield from down_chunk(c, first, r, FFN_BANKS, store_shared(p, c), shh, shl)
            low_read[r] = last_down[0]

        EARLY_GROUPS = GROUPS - 2
        offset[0] = routing_start
        probs = at("probs", [P, GROUPS, E], F32, 4)
        key = at("key", [P, GROUPS, E], F32, 4)
        onehot = at("onehot", [P, GROUPS, TOPK, E], F32, 4)
        onehotb = at("onehotb", [P, GROUPS, TOPK * E], BF16, 2)
        earlier = at("earlier", [P, GROUPS, TOPK * E], BF16, 2)
        chosen = at("chosen", [P, GROUPS, TOPK * E], F32, 4)
        rank_of_e = at("rank_of_e", [P, E], F32, 4)
        first_slot = at("first_slot", [P, E], F32, 4)
        red = at("red", [P, GROUPS], F32, 4)
        rsum = at("rsum", [P, GROUPS], F32, 4)
        weight = at("weight", [P, GROUPS, TOPK], F32, 4)
        place = at("place", [P, GROUPS, TOPK], F32, 4)
        place0 = at("place0", [P, GROUPS, TOPK], F32, 4)
        keep = at("keep", [P, GROUPS, TOPK], F32, 4)
        slot_of = at("slot_of", [P, GROUPS, TOPK], I32, 4)
        entry = at("entry", [P, GROUPS, TOPK, 2], I32, 4)
        empty = at("empty", [P, E * CH, 2], I32, 4)
        zrows = at("zrows", [P, 2 * D], BF16, 2)

        s_iota = signal("s_iota")
        s_fill = dma_signal("s_fill")
        iotas, filled = [], []

        def start_routing():
            pool.wait(st_done[EARLY_GROUPS - 1])
            pool.do(gp.iota, rank_of_e[:, :], pattern=[[-1, E]], base=E, channel_multiplier=0,
                    allow_small_or_imprecise_dtypes=True, done=s_iota)
            pool.do(gp.iota, first_slot[:, :], pattern=[[SLOTS, E]], base=0, channel_multiplier=0,
                    allow_small_or_imprecise_dtypes=True, done=s_iota)
            pool.do(gp.memset, empty[:, :, 1], 0, done=s_iota)
            pool.do(gp.iota, empty[:, :, 0], pattern=[[0, E * CH]], base=T, channel_multiplier=1, done=s_iota)
            for k in range(TOPK):
                pool.do(gp.iota, entry[:, :, k, 0], pattern=[[P, GROUPS]], base=0, channel_multiplier=1, done=s_iota)
            pool.do(gp.memset, zrows[:, :], 0.0, done=s_iota)
            iotas.append(s_iota.now())
            sp.wait(*iotas)
            sp.do(nc.sync.dma_start, table.rearrange("(e p c) two -> p e (c two)", p=P, c=CH),
                  empty[:, :, :].rearrange("p (e c) two -> p e (c two)", e=E), done=s_fill)
            sp.do(nc.sync.dma_start, xn_rows[T:T + P, :], zrows[:, :], done=s_fill)
            sp.do(nc.sync.dma_start, out[T:T + P, :], zrows[:, :].bitcast(F32), done=s_fill)
            filled.append(s_fill.now())

        s_place = signal("s_place")
        entries_ready = {}

        def route(first, last):
            n, gs = last - first, slice(first, last)

            def wide(ap):
                return ap[:, gs].unsqueeze(2).to_broadcast([P, n, E])

            def over_groups(ap):
                return ap.unsqueeze(1).to_broadcast([P, n, E])

            dve.wait(*iotas, s_logit.now())
            some, some_keys = probs[:, gs, :], key[:, gs, :]
            step(dv.tensor_reduce, red[:, gs], logits[:, gs, :], X_AXIS, ALU.max)
            yield
            m = step(dv.tensor_tensor, some, logits[:, gs, :], wide(red), ALU.subtract)
            yield
            act.wait(m)
            m = act.do(ac.activation, some, some, ACT.Exp, done=s_act)
            yield
            dve.wait(m)
            step(dv.tensor_reduce, rsum[:, gs], some, X_AXIS, ALU.add)
            yield
            step(dv.reciprocal, rsum[:, gs], rsum[:, gs])
            yield
            step(dv.tensor_tensor, some, some, wide(rsum), ALU.mult)
            yield
            for k in range(TOPK):
                step(dv.tensor_reduce, weight[:, gs, k], some, X_AXIS, ALU.max)
                yield
                step(dv.tensor_tensor, some_keys, some, wide(weight[:, :, k]), ALU.is_ge)
                yield
                step(dv.tensor_tensor, some_keys, some_keys, over_groups(rank_of_e[:, :]), ALU.mult)
                yield
                step(dv.tensor_reduce, red[:, gs], some_keys, X_AXIS, ALU.max)
                yield
                step(dv.tensor_tensor, onehot[:, gs, k, :], over_groups(rank_of_e[:, :]), wide(red), ALU.is_equal)
                yield
                if k == 0:
                    step(dv.scalar_tensor_tensor, some, onehot[:, gs, 0, :], -2.0, some, ALU.mult, ALU.add)
                    yield
            step(dv.tensor_copy, onehotb[:, gs, :], onehot[:, gs, :, :].rearrange("p g k e -> p g (k e)"))
            yield "counted"
            if first == 0:
                step(dv.memset, earlier[:, 0, :], 0.0)
                yield
            for g in range(max(first, 1), last):
                step(dv.tensor_tensor, earlier[:, g, :], earlier[:, g - 1, :], onehotb[:, g - 1, :], ALU.add)
                yield
            counted = s_dve.now()
            for _ in range(6 if first == 0 else 0):
                yield
            pe.wait(counted, bank_free[5])
            n_all = n * TOPK * E
            pe.do(mm, bank(5)[:, 0:n_all], before[:, :], onehotb[:, gs, :].rearrange("p g k -> p (g k)"), start=True, stop=False)
            m = pe.do(mm, bank(5)[:, 0:n_all], ones[:, :], earlier[:, gs, :].rearrange("p g k -> p (g k)"), start=False, stop=True, done=s_place)
            dve.wait(m)
            gk = n * TOPK
            oh = onehot[:, gs, :, :].rearrange("p g k e -> p (g k e)")
            ch = chosen[:, gs, :].rearrange("p g k -> p (g k)")
            places, bases = (a[:, gs, :].rearrange("p g k -> p (g k)") for a in (place, place0))
            step(dv.tensor_tensor, ch, bank(5)[:, 0:n_all], oh, ALU.mult)
            yield
            bank_free[5] = s_dve.now()
            step(dv.tensor_reduce, places, ch.rearrange("p (a e) -> p a e", e=E), X_AXIS, ALU.add)
            yield
            step(dv.tensor_tensor, ch.rearrange("p (a e) -> p a e", e=E), oh.rearrange("p (a e) -> p a e", e=E),
                 first_slot[:, :].unsqueeze(1).to_broadcast([P, gk, E]), ALU.mult)
            yield
            step(dv.tensor_reduce, bases, ch.rearrange("p (a e) -> p a e", e=E), X_AXIS, ALU.add)
            yield
            step(dv.tensor_scalar, keep[:, gs, :], place[:, gs, :], float(CAP), float(DROPPED), ALU.is_ge, ALU.mult)
            yield
            step(dv.tensor_tensor, place[:, gs, :], place[:, gs, :], place0[:, gs, :], ALU.add)
            yield
            step(dv.tensor_tensor, place[:, gs, :], place[:, gs, :], keep[:, gs, :], ALU.add)
            yield
            step(dv.tensor_copy, slot_of[:, gs, 0], place[:, gs, 0])
            yield
            step(dv.tensor_scalar, slot_of[:, gs, 1], place[:, gs, 1], float(CAP), None, ALU.add)
            yield
            entries_ready[first] = step(dv.tensor_copy, entry[:, gs, :, 1].bitcast(F32), weight[:, gs, :])
            yield

        s_scatter = dma_signal("s_scatter")

        def scatter(first, last):
            pool.wait(entries_ready[first], *iotas, *filled)
            for g in range(first, last):
                for k in range(TOPK):
                    pool.do(gp.indirect_dma_start, out=table, out_offset=bass.IndirectOffsetOnAxis(ap=slot_of[:, g, k:k + 1], axis=0),
                            in_=entry[:, g, k, :], in_offset=None, bounds_check=E * SLOTS - 1, oob_is_err=False, done=s_scatter)
                    yield

        def step_of(streams):
            while streams and next(streams[0], "over") == "over":
                streams.pop(0)

        EARLY = 8

        def s_bank(w, i):
            banks = [0, 6, 1, 7] if w < 2 else [0, 1]
            return banks[i % len(banks)]

        def without_exponentials(w):
            values = [weighted_values(2 * w - 1, QT - 1, *PV_BANKS[1])] if w >= 1 else []
            side = [finish_attention(2 * w - 1, *PV_BANKS[1])] if w >= 1 else []
            for k, g in enumerate((2 * w, 2 * w + 1)):
                tokens = [transpose_tokens(g - 2, 2 if k else 5)] if w >= 1 else []
                if g < GROUPS:
                    transpose_values(g, 4)
                for i in range(EARLY if w and k == 0 and g < GROUPS else 0, GH * QT):
                    if g < GROUPS:
                        score_max(g, i, s_bank(w, i))
                    if values:
                        step_of(values)
                        step_of(values)
                    else:
                        step_of(side)
                    if w < 2 and i % 8 == 3:
                        next(weights, None)
                    if i >= 12 or (k and not side):
                        step_of(tokens)
                    if k == 0 and i == 15 and g + 2 < GROUPS:
                        load_group(g + 2)
                    if k == 1 and g < GROUPS:
                        if i == 0:
                            max_parts(g - 1)
                        if i == 4:
                            for _ in max_rows(g - 1, 4):
                                pass
                    if k and i == 11:
                        for rest in side:
                            for _ in rest:
                                pass
                        if g + 2 < GROUPS:
                            load_group(g + 2)
                    if i % 2:
                        yield
                for rest in tokens:
                    for _ in rest:
                        pass
            if g < GROUPS:
                max_parts(g)

        def with_exponentials(w):
            for k, g in enumerate((2 * w, 2 * w + 1)):
                if k == 1:
                    side = [finish_attention(g - 1, *PV_BANKS[0])]
                    if w == LAST - 1:
                        side.append(early_routing)
                elif w < LAST - 1:
                    side = [prepare(n) for n in (g + 2, g + 3)]
                else:
                    start_routing()
                    side = []
                values = []
                rows = max_rows(g + 1, 3)
                for i in range(GH * QT):
                    exponentials(g, i, s_bank(w, i))
                    if k == 0 and i >= 4:
                        next(rows, None)
                    if i >= 4 * k:
                        for _ in range(3 if k and i < 6 else 2):
                            step_of(side)
                    if g == GROUPS - 2:
                        next(early_routing)
                        next(early_routing)
                    if k == 1 and i >= GH * QT - EARLY and g + 1 < GROUPS:
                        score_max(g + 1, i - (GH * QT - EARLY), 5 - i % 2)
                    yield
                    if i % GH == 1 and (i > GH or k == 1):
                        n, t = divmod(g * QT + i // GH - 1, QT)
                        values = [weighted_values(n, t, *PV_BANKS[n % 2])]
                    for _ in range((0, 1, 2, 2)[i % GH]):
                        step_of(values)
                for rest in side:
                    for _ in rest:
                        pass

        def together(main, other, ratio, all_of_other=True):
            owed = 0.0
            for _ in main:
                owed += ratio
                while owed >= 1:
                    owed -= 1
                    next(other, None)
            if all_of_other:
                for _ in other:
                    pass

        PV_BANKS = [(4, 5), (2, 3)]
        weights = shared_weights()
        load_group(0)
        load_group(1)
        s_small = dma_signal("s_small")
        sp.do(nc.sync.dma_start, scale_i[:, :], itok.rearrange("(a b) -> a b", a=1).partition_broadcast(P).rearrange("p a b -> p (a b)"), done=s_small)
        sp.do(nc.sync.dma_start, gate[:, :, :], gate_w.rearrange("(k p) e -> p k e", p=P), done=s_small)
        sp.do(nc.sync.dma_start, b1rows[:, :], b1.rearrange("e (c p) -> (e c) p", p=P), done=s_small)
        sp.do(nc.sync.dma_start, sb1rows[:, :], sb1.rearrange("(c p) -> c p", p=P), done=s_small)
        sp.do(nc.sync.dma_start, b2f[0:E, :], b2, done=s_small)
        sp.do(nc.sync.dma_start, b2f[E:E + 1, :], sb2.rearrange("(a d) -> a d", a=1), done=s_small)
        loaded_small = s_small.now()
        for g in range(2):
            for _ in prepare(g):
                pass
            if g == 0:
                next(weights)
        s_scale = signal("s_scale")
        pool.wait(s_rstd.now())
        for i in range(NS):
            fill(KS[i][96:P, :, :], 1.0)
        fill(wus[96:P, :], 0.0)
        for i in range(2):
            fill(low[i][96:P, :], 1.0)
        filled_late.append(s_pool.now())
        dve.wait(loaded_small)
        m = dve.do(dv.tensor_copy, scale_f[:, :], scale_i[:, :], done=s_dve)
        act.wait(m)
        m = act.do(ac.activation, scales[:, :], scale_f[:, :], ACT.Ln, done=s_act)
        dve.wait(m)
        m_scale = dve.do(dv.tensor_scalar, scales[:, :], scales[:, :], SCALE, None, ALU.mult, done=s_scale)
        act.wait(m_scale)
        step(dv.tensor_copy, b2parts[:, 0, :], b2f[:, :])
        step(dv.tensor_tensor, b2f[:, :], b2f[:, :], b2parts[:, 0, :], ALU.subtract)
        step(dv.tensor_copy, b2parts[:, 1, :], b2f[:, :])
        m_b2 = step(dv.tensor_tensor, b2parts[:, 2, :], b2f[:, :], b2parts[:, 1, :], ALU.subtract)
        s_bias = signal("s_bias")
        s_biasc = signal("s_biasc")
        pe.wait(loaded_small)
        pe.do(tr, bank(5)[:, 0:P], b1rows[:, :], ident[:, :])
        m = pe.do(tr, bank(5)[:, P:P + FB], sb1rows[:, :], ident[0:FB, 0:FB], done=s_bias)
        dve.wait(m)
        dve.do(dv.tensor_copy, b1cols[:, :], bank(5)[:, 0:P], done=s_biasc)
        m_biascols = dve.do(dv.tensor_copy, sb1cols[:, :], bank(5)[:, P:P + FB], done=s_biasc)
        act.wait(m_biascols)
        dve.wait(filled_late[0])
        sp.wait(filled_late[0])
        bank_free[5] = m_biascols
        b2_parts_ready[:] = [m_b2]
        LAST = GROUPS // 2
        early_routing = route(0, EARLY_GROUPS)
        nothing = iter(())
        UP_RATE = 22 / 12
        for w in range(LAST):
            p = w - 2
            if p == 0:
                for _ in weights:
                    pass
                act.wait(s_wlog.now(), s_whi.now())
                pool.wait(s_wlog.now(), s_whi.now())
            together(without_exponentials(w), shared_up(p) if p >= 0 else nothing, UP_RATE)
            together(with_exponentials(w), shared_down(p) if p >= 0 else nothing, 1)

        def beside(*streams):
            streams = list(streams)
            while streams:
                streams = [s for s in streams if next(s, "over") != "over"]
                yield

        together(without_exponentials(LAST), beside(shared_up(6), scatter(0, EARLY_GROUPS)), 1)
        together(shared_down(6), route(EARLY_GROUPS, GROUPS), 2)
        for _ in scatter(EARLY_GROUPS, GROUPS):
            pass
        attention_over = [s_pv.now(), s_ST.now(), s_x2t.now(), s_logit.now(), s_xt.now(), s_out.now(),
                          s_x2r.now(), s_ph.now(), s_pl.now(), s_mrowc.now(), s_gate.now()]
        attention_over += [s.now() for s in s_x1st + s_x2st + s_stack]
        for queue in (sp, act, dve, pool):
            queue.wait(*attention_over)

        s_gather = dma_signal("s_gather")
        s_et, s_etc_h, s_etc_l = signal("s_et"), signal("s_etc_h"), signal("s_etc_l")
        HALVES = [(0, CAP), (CAP, CAP)]
        E_UNITS, E_YBANKS, E_TR = [0, 2], [4, 5], [6, 7]
        rows_stored = [s.now() for s in s_x2st]
        expert_x, et_read = {}, {}

        def gather(e):
            pool.wait(m_slots, *filled, *rows_stored)
            if e:
                pool.wait(et_mark[e - 1])
            for c in range(CH):
                pool.do(gp.indirect_dma_start, out=xg[:, c, :], out_offset=None, in_=xn_rows,
                        in_offset=bass.IndirectOffsetOnAxis(ap=slots[:, e, c, 0:1], axis=0), bounds_check=T + P - 1,
                        oob_is_err=True, done=s_gather)
            gathered[e] = s_gather.now()

        gathered, et_mark = {}, {}
        SPREAD = 6

        def transpose_slots(e, banks):
            pe.wait(gathered[e])
            if e >= 2:
                act.wait(et_read[e - 2])
                dve.wait(et_read[e - 2])
            for c in range(CH):
                b = banks[c % 2]
                pe.wait(bank_free[b])
                view = bank(b).bitcast(BF16)
                for j in range(2 * KB):
                    pe.do(tr, view[:, j * P:j * P + P], xg[:, c, j * P:j * P + P], identb[:, :], done=s_et if j == 2 * KB - 1 else None)
                m = s_et.now()
                dst = slice(c * P, c * P + P)
                src = view.rearrange("p (a k t) -> p a k t", a=2, k=KB)
                act.wait(m)
                mh = act.do(ac.activation, eth[e % 2][:, :, dst], src[:, 0], ACT.Copy, done=s_etc_h)
                act.wait(mh)
                ml = act.do(ac.activation, etl[e % 2][:, :, dst], src[:, 1], ACT.Copy, done=s_etc_l)
                bank_free[b] = ml
                for _ in range(SPREAD if e else SPREAD - 2):
                    yield
            et_mark[e] = s_et.now()
            expert_x[e] = [s_etc_h.now(), s_etc_l.now()]
            yield

        def store_expert(e, c):
            def store(n, b):
                y = yout[n % 3]
                act.wait(m_slots)
                m = act.do(ac.activation, y[:, :], bank(b), ACT.Copy, scale=slots[:, e, c, 1:2].bitcast(F32), done=s_y)
                pool.wait(m, *filled, *[s.now() for s in s_yst])
                return m, pool.do(gp.indirect_dma_start, out=out, out_offset=bass.IndirectOffsetOnAxis(ap=slots[:, e, c, 0:1], axis=0),
                                  in_=y[:, :], in_offset=None, bounds_check=T + P - 1, oob_is_err=True, compute_op=ALU.add,
                                  done=s_yst[n % 3])
            return store

        stage_free.clear()
        for queue in (pe, act, dve, pool, sp):
            queue.wait(*attention_over)
        stages = [s[:, :] for s in stage]
        order = [(e, f, w[e], q) for e in range(E) for f, w in ((w1_quarter, w1), (w2_quarter, w2)) for q in range(4)]
        LEAD = NST - 1
        pending = []

        def next_quarter(written_over):
            while len(pending) < len(order) and len(pending) <= quarter_at[0] + LEAD:
                _, f, w, q = order[len(pending)]
                pending.append(f(stages, w, q, []))
            quarter_at[0] += 1
            act.wait(written_over)
            dve.wait(written_over)
            return pending[quarter_at[0] - 1]()

        quarter_at = [0]

        def first_weights():
            w1_ready["next"] = []
            rank_down_weights(wd[0], s_up.now())
            for q in range(4):
                for _ in range(6):
                    yield
                w1_ready["next"].append(next_quarter(s_up.now()))

        s_table = dma_signal("s_table")
        sp.wait(s_scatter.now())
        m_slots = sp.do(nc.sync.dma_start, slots[:, :, :, :].rearrange("p e c two -> p e (c two)"),
                        table.rearrange("(e p c) two -> p e (c two)", p=P, c=CH), done=s_table)
        gather(0)
        for _ in shared_up(7, False):
            pass
        turning = transpose_slots(0, E_YBANKS)
        for i, _ in enumerate(beside(shared_down(7), first_weights())):
            if i >= 8:
                next(turning, None)
        for _ in turning:
            pass
        for e in range(E):
            w1_ready["now"] = w1_ready["next"]
            pe.wait(*expert_x[e])
            hi, lo = eth[e % 2], etl[e % 2]
            w2_free = last_down[0]
            r = rank_features(hi, lo, HALVES, E_UNITS)
            rank_up_weights(wu[e], e, w2_free)
            if e + 1 < E:
                gather(e + 1)
            first = count["up"]
            w2_ready["now"] = []
            for fb in range(FB):
                if fb % 4 == 0:
                    w2_ready["now"].append(next_quarter(w2_free))
                up_block(hi, lo, HALVES, fb, E_UNITS, b1cols[:, e * FB + fb:e * FB + fb + 1], hh, hl)
            et_read[e] = s_up.now()
            w1_free = s_up.now()
            w1_ready["next"] = []
            for c in range(CH):
                if c < 4 and e + 1 < E:
                    w1_ready["next"].append(next_quarter(w1_free))
                if c == 2 and e + 1 < E:
                    turning = transpose_slots(e + 1, E_TR)
                for _ in down_chunk(c, first, r, E_YBANKS, store_expert(e, c), hh, hl):
                    if c >= 2 and e + 1 < E:
                        next(turning, None)
                if c == 1 and e + 1 < E:
                    rank_down_weights(wd[e + 1], w1_free)
            low_read[r] = last_down[0]
        sp.wait(*[s.now() for s in s_yst + s_x1st + s_x2st + [s_fill, s_scatter]])

        block = stack.enter_context(nc.Block())

        @block.sync
        def _(engine):
            sp.issue(engine)

        @block.gpsimd
        def _(engine):
            pool.issue(engine)

        @block.scalar
        def _(engine):
            act.issue(engine)

        @block.vector
        def _(engine):
            dve.issue(engine)

        @block.tensor
        def _(engine):
            pe.issue(engine)


_INPUTS = ["x", "ctx_2048", "itok_B_779_1933", "L0_ffn_gate_w", "L0_ffn_w1", "L0_ffn_b1", "L0_ffn_w2", "L0_ffn_b2",
           "L0_ffn_wd", "L0_ffn_wu", "L0_ffn_sw1", "L0_ffn_sb1", "L0_ffn_sw2", "L0_ffn_sb2", "L0_ffn_swd", "L0_ffn_swu"]


def kernel(**inputs):
    import concourse.bacc as bacc
    from concourse.bass_utils import run_bass_kernel_spmd

    nc = bacc.Bacc("TRN2", target_bir_lowering=False, num_devices=1, dynamic_dma_scratch_size=8192)
    arrays, args = {}, []
    for name in _INPUTS:
        a = np.ascontiguousarray(inputs[name])
        arrays[f"in_{name}"] = a
        args.append(nc.dram_tensor(f"in_{name}", a.shape, mybir.dt.from_np(a.dtype), kind="ExternalInput").ap())
    out = nc.dram_tensor("out_rows", (T + P, D), F32, kind="ExternalOutput").ap()
    build(nc, *args, out)
    r = run_bass_kernel_spmd(nc, [arrays], core_ids=[0])
    return r.results[0]["out_rows"][:T].reshape(B, C, L)
```
